# Optimizing a Trainium2 kernel written in Bass

```python
import numpy as np
import jax
import jax.numpy as jnp

def _softmax(x, axis=-1):
    return jax.nn.softmax(x, axis=axis)

def _gelu(x):
    return jax.nn.gelu(x, approximate=True)

def _silu(x):
    return jax.nn.silu(x)

def _sigmoid(x):
    return jax.nn.sigmoid(x)

def _layernorm(x, axis=-1, eps=1e-05):
    m = jnp.mean(x, axis=axis, keepdims=True)
    v = jnp.var(x, axis=axis, keepdims=True)
    return (x - m) / jnp.sqrt(v + eps)

def _scatter_add(tgt, idx, src, axis=0):
    return tgt.at[idx].add(src)

def _segment_sum(src, seg, n):
    return jax.ops.segment_sum(src, seg, n)
kernel_name = 'mk_dlrm_tower_d1_rec_r8_f7dd68'

def setup_inputs(seed: int=0):
    np.random.seed(seed)
    _w = jnp.asarray

    def _rec_inputs():
        import jax
        import jax.numpy as jnp
        _tk = jax.random.key(seed)
        dense_ctx = jax.random.normal(jax.random.fold_in(_tk, 190), (2048, 16), jnp.float32)
        ids = jnp.stack([jax.random.randint(jax.random.fold_in(_tk, 200 + f), (2048,), 0, v, jnp.int32) for f, v in enumerate([12500, 1000, 1250, 125000, 1250, 12500, 125000, 125000, 12500, 1000, 12500, 1000, 1000, 12500, 1000, 125000, 125000, 1000, 1250, 12500, 12500, 1000, 1000, 1250, 1250, 125000])], axis=1)
        tbl_0 = 0.05 * jax.random.normal(jax.random.fold_in(_tk, 500 + 0), (12500, 32), jnp.float32)
        tbl_1 = 0.05 * jax.random.normal(jax.random.fold_in(_tk, 500 + 1), (1000, 32), jnp.float32)
        tbl_2 = 0.05 * jax.random.normal(jax.random.fold_in(_tk, 500 + 2), (1250, 32), jnp.float32)
        tbl_3 = 0.05 * jax.random.normal(jax.random.fold_in(_tk, 500 + 3), (125000, 32), jnp.float32)
        tbl_4 = 0.05 * jax.random.normal(jax.random.fold_in(_tk, 500 + 4), (1250, 32), jnp.float32)
        tbl_5 = 0.05 * jax.random.normal(jax.random.fold_in(_tk, 500 + 5), (12500, 32), jnp.float32)
        tbl_6 = 0.05 * jax.random.normal(jax.random.fold_in(_tk, 500 + 6), (125000, 32), jnp.float32)
        tbl_7 = 0.05 * jax.random.normal(jax.random.fold_in(_tk, 500 + 7), (125000, 32), jnp.float32)
        tbl_8 = 0.05 * jax.random.normal(jax.random.fold_in(_tk, 500 + 8), (12500, 32), jnp.float32)
        tbl_9 = 0.05 * jax.random.normal(jax.random.fold_in(_tk, 500 + 9), (1000, 32), jnp.float32)
        tbl_10 = 0.05 * jax.random.normal(jax.random.fold_in(_tk, 500 + 10), (12500, 32), jnp.float32)
        tbl_11 = 0.05 * jax.random.normal(jax.random.fold_in(_tk, 500 + 11), (1000, 32), jnp.float32)
        tbl_12 = 0.05 * jax.random.normal(jax.random.fold_in(_tk, 500 + 12), (1000, 32), jnp.float32)
        tbl_13 = 0.05 * jax.random.normal(jax.random.fold_in(_tk, 500 + 13), (12500, 32), jnp.float32)
        tbl_14 = 0.05 * jax.random.normal(jax.random.fold_in(_tk, 500 + 14), (1000, 32), jnp.float32)
        tbl_15 = 0.05 * jax.random.normal(jax.random.fold_in(_tk, 500 + 15), (125000, 32), jnp.float32)
        tbl_16 = 0.05 * jax.random.normal(jax.random.fold_in(_tk, 500 + 16), (125000, 32), jnp.float32)
        tbl_17 = 0.05 * jax.random.normal(jax.random.fold_in(_tk, 500 + 17), (1000, 32), jnp.float32)
        tbl_18 = 0.05 * jax.random.normal(jax.random.fold_in(_tk, 500 + 18), (1250, 32), jnp.float32)
        tbl_19 = 0.05 * jax.random.normal(jax.random.fold_in(_tk, 500 + 19), (12500, 32), jnp.float32)
        tbl_20 = 0.05 * jax.random.normal(jax.random.fold_in(_tk, 500 + 20), (12500, 32), jnp.float32)
        tbl_21 = 0.05 * jax.random.normal(jax.random.fold_in(_tk, 500 + 21), (1000, 32), jnp.float32)
        tbl_22 = 0.05 * jax.random.normal(jax.random.fold_in(_tk, 500 + 22), (1000, 32), jnp.float32)
        tbl_23 = 0.05 * jax.random.normal(jax.random.fold_in(_tk, 500 + 23), (1250, 32), jnp.float32)
        tbl_24 = 0.05 * jax.random.normal(jax.random.fold_in(_tk, 500 + 24), (1250, 32), jnp.float32)
        tbl_25 = 0.05 * jax.random.normal(jax.random.fold_in(_tk, 500 + 25), (125000, 32), jnp.float32)
        _rk = jax.random.fold_in(_tk, 7)
        W_top1 = 0.0606339 * jax.random.normal(jax.random.fold_in(_tk, 801), (272, 512), jnp.float32)
        W_top2 = 0.0441942 * jax.random.normal(jax.random.fold_in(_tk, 802), (512, 256), jnp.float32)
        W_top3 = 0.0625 * jax.random.normal(jax.random.fold_in(_tk, 803), (256, 1), jnp.float32)
        b_top1 = jnp.zeros((512,), jnp.float32)
        b_top2 = jnp.zeros((256,), jnp.float32)
        return (dense_ctx, ids, tbl_0, tbl_1, tbl_2, tbl_3, tbl_4, tbl_5, tbl_6, tbl_7, tbl_8, tbl_9, tbl_10, tbl_11, tbl_12, tbl_13, tbl_14, tbl_15, tbl_16, tbl_17, tbl_18, tbl_19, tbl_20, tbl_21, tbl_22, tbl_23, tbl_24, tbl_25, W_top1, b_top1, W_top2, b_top2, W_top3)
    dense_ctx, ids, tbl_0, tbl_1, tbl_2, tbl_3, tbl_4, tbl_5, tbl_6, tbl_7, tbl_8, tbl_9, tbl_10, tbl_11, tbl_12, tbl_13, tbl_14, tbl_15, tbl_16, tbl_17, tbl_18, tbl_19, tbl_20, tbl_21, tbl_22, tbl_23, tbl_24, tbl_25, W_top1, b_top1, W_top2, b_top2, W_top3 = _rec_inputs()

    def _L0_rec_setup():
        import jax, jax.numpy as jnp
        import numpy as np
        M_FIELDS = 26
        H1 = 128
        H2 = 128
        BATCH = 256
        EMB_K = 32

        def _cin_layer(x_prev, x0, W, b):
            return jnp.einsum('bik,bjk,hij->bhk', x_prev, x0, W) + b[None, :, None]
        key = jax.random.key(seed)
        k0, k1, k2, k3, k4 = jax.random.split(key, 5)
        inputs = jax.random.normal(k0, (BATCH, M_FIELDS, EMB_K), dtype=jnp.float32)
        W1 = jax.random.normal(k1, (H1, M_FIELDS, M_FIELDS), dtype=jnp.float32) * 0.05
        b1 = jax.random.normal(k2, (H1,), dtype=jnp.float32) * 0.05
        W2 = jax.random.normal(k3, (H2, H1, M_FIELDS), dtype=jnp.float32) * 0.05
        b2 = jax.random.normal(k4, (H2,), dtype=jnp.float32) * 0.05
        return {'inputs': inputs, 'W1': W1, 'b1': b1, 'W2': W2, 'b2': b2}
    _L0_rec_all = _L0_rec_setup()
    _L0_rec_in = {k: v for k, v in _L0_rec_all.items() if k in ('W1', 'b1', 'W2', 'b2')}
    del _L0_rec_all
    return {'dense_ctx': dense_ctx, 'ids': ids, 'tbl_0': tbl_0, 'tbl_1': tbl_1, 'tbl_2': tbl_2, 'tbl_3': tbl_3, 'tbl_4': tbl_4, 'tbl_5': tbl_5, 'tbl_6': tbl_6, 'tbl_7': tbl_7, 'tbl_8': tbl_8, 'tbl_9': tbl_9, 'tbl_10': tbl_10, 'tbl_11': tbl_11, 'tbl_12': tbl_12, 'tbl_13': tbl_13, 'tbl_14': tbl_14, 'tbl_15': tbl_15, 'tbl_16': tbl_16, 'tbl_17': tbl_17, 'tbl_18': tbl_18, 'tbl_19': tbl_19, 'tbl_20': tbl_20, 'tbl_21': tbl_21, 'tbl_22': tbl_22, 'tbl_23': tbl_23, 'tbl_24': tbl_24, 'tbl_25': tbl_25, 'W_top1': W_top1, 'b_top1': b_top1, 'W_top2': W_top2, 'b_top2': b_top2, 'W_top3': W_top3, 'L0_rec_W1': _L0_rec_in['W1'], 'L0_rec_b1': _L0_rec_in['b1'], 'L0_rec_W2': _L0_rec_in['W2'], 'L0_rec_b2': _L0_rec_in['b2']}

def reference(dense_ctx, ids, tbl_0, tbl_1, tbl_2, tbl_3, tbl_4, tbl_5, tbl_6, tbl_7, tbl_8, tbl_9, tbl_10, tbl_11, tbl_12, tbl_13, tbl_14, tbl_15, tbl_16, tbl_17, tbl_18, tbl_19, tbl_20, tbl_21, tbl_22, tbl_23, tbl_24, tbl_25, W_top1, b_top1, W_top2, b_top2, W_top3, L0_rec_W1, L0_rec_b1, L0_rec_W2, L0_rec_b2):
    import jax
    import jax.numpy as jnp

    def _L0_rec_ref(inputs, W1, b1, W2, b2):
        import jax, jax.numpy as jnp
        import numpy as np
        M_FIELDS = 26
        H1 = 128
        H2 = 128
        BATCH = 256
        EMB_K = 32

        def _cin_layer(x_prev, x0, W, b):
            return jnp.einsum('bik,bjk,hij->bhk', x_prev, x0, W) + b[None, :, None]
        x1 = _cin_layer(inputs, inputs, W1, b1)
        x2 = _cin_layer(x1, inputs, W2, b2)
        res = jnp.concatenate([x1, x2], axis=1)
        return jnp.sum(res, axis=-1)
    e = jnp.stack([tbl_0[ids[:, 0]], tbl_1[ids[:, 1]], tbl_2[ids[:, 2]], tbl_3[ids[:, 3]], tbl_4[ids[:, 4]], tbl_5[ids[:, 5]], tbl_6[ids[:, 6]], tbl_7[ids[:, 7]], tbl_8[ids[:, 8]], tbl_9[ids[:, 9]], tbl_10[ids[:, 10]], tbl_11[ids[:, 11]], tbl_12[ids[:, 12]], tbl_13[ids[:, 13]], tbl_14[ids[:, 14]], tbl_15[ids[:, 15]], tbl_16[ids[:, 16]], tbl_17[ids[:, 17]], tbl_18[ids[:, 18]], tbl_19[ids[:, 19]], tbl_20[ids[:, 20]], tbl_21[ids[:, 21]], tbl_22[ids[:, 22]], tbl_23[ids[:, 23]], tbl_24[ids[:, 24]], tbl_25[ids[:, 25]]], axis=1)
    z = _L0_rec_ref(e, L0_rec_W1, L0_rec_b1, L0_rec_W2, L0_rec_b2)
    z = z.reshape(z.shape[0], -1)
    h = jnp.concatenate([z, dense_ctx], axis=1)
    h = jnp.maximum(h @ W_top1 + b_top1, 0.0)
    h = jnp.maximum(h @ W_top2 + b_top2, 0.0)
    y = h @ W_top3
    return y

_drawn_inputs = setup_inputs


def setup_inputs(seed=0):
    import zlib

    import numpy as np

    out = dict(_drawn_inputs(seed))
    spreads = {'b_top1': (0.0, 2.0), 'b_top2': (0.0, 0.8)}
    factors = {'tbl_0': 8.0,
     'tbl_1': 8.0,
     'tbl_2': 8.0,
     'tbl_3': 8.0,
     'tbl_4': 8.0,
     'tbl_5': 8.0,
     'tbl_6': 8.0,
     'tbl_7': 8.0,
     'tbl_8': 8.0,
     'tbl_9': 8.0,
     'tbl_10': 8.0,
     'tbl_11': 8.0,
     'tbl_12': 8.0,
     'tbl_13': 8.0,
     'tbl_14': 8.0,
     'tbl_15': 8.0,
     'tbl_16': 8.0,
     'tbl_17': 8.0,
     'tbl_18': 8.0,
     'tbl_19': 8.0,
     'tbl_20': 8.0,
     'tbl_21': 7.878,
     'tbl_22': 8.0,
     'tbl_23': 8.0,
     'tbl_24': 8.0,
     'tbl_25': 8.0,
     'L0_rec_W1': 8.0,
     'L0_rec_W2': 4.233,
     'dense_ctx': 6.251}
    for name, (base, spread) in spreads.items():
        noise = np.random.default_rng([zlib.crc32(name.encode()), seed]).standard_normal(out[name].shape)
        drawn = base * np.exp(spread * noise) if base else spread * noise
        out[name] = jnp.asarray(drawn.astype(out[name].dtype))
    for name, factor in factors.items():
        out[name] = (out[name] * factor).astype(out[name].dtype)
    return out
```

```python
import concourse.bass as bass
from concourse import mybir
from contextlib import ExitStack

FIELDS = 26
EMB = 32
HC = 128
NX, NY, NZ = 5, 6, 15
P = 128
QUADS = P // EMB


def tri(n):
    return n * (n + 1) // 2


COL_XX = 0
COL_XY = COL_XX + tri(NX)
COL_XZ = COL_XY + NX * NY
COL_YZ = COL_XZ + NX * NZ
COL_YY = COL_YZ + NY * NZ
COL_ZZ = COL_YY + tri(NY)
COL_1 = COL_ZZ + tri(NZ)
PAIRS = COL_1 + 1
X0, Y0, Z0 = 0, NX, NX + NY


def tri_row(n, a):
    return a * n - a * (a - 1) // 2


class Chunk:
    def __init__(self, name, first, last, others, per_bank):
        self.name, self.first, self.pairs = name, first, last - first
        self.others = others
        self.per_bank = per_bank
        self.banks = EMB // per_bank


CHUNKS = [
    Chunk("a", COL_ZZ, PAIRS, 1 + FIELDS, 4),
    Chunk("b", COL_YZ, COL_ZZ, 1 + NX + NY, 8),
    Chunk("c", COL_XX, COL_YZ, 1 + NX, 16),
]
FILLS = sum(c.banks for c in CHUNKS)
AFTER = [sum(c.banks for c in CHUNKS[:i + 1]) for i in range(3)]
RING = 4
PAIRED = 2


def dlrm_tower(nc, dense_t, ids, tables, w_top1, b_top1, w_top2, b_top2, w_top3, w1, b1, w2, b2, y):
    fp32 = mybir.dt.float32
    i32 = mybir.dt.int32
    ALU = mybir.AluOpType
    ACT = mybir.ActivationFunctionType

    batch = dense_t.shape[1]
    n_dense = dense_t.shape[0]
    tiles = batch // P
    steps = tiles // PAIRED
    rows = PAIRED * P
    m1 = w_top1.shape[1] // P
    m2 = w_top2.shape[1] // P
    assert FILLS * PAIRED % RING == 0 and 2 * HC + n_dense == w_top1.shape[0]

    ctx = ExitStack()
    with ctx:
        def sb(name, shape, dt=fp32):
            return ctx.enter_context(nc.sbuf_tensor(name, shape, dt))

        def ps(name, shape):
            return ctx.enter_context(nc.psum_tensor(name, shape, fp32))

        def sem(name):
            return ctx.enter_context(nc.semaphore(name))

        ids_all = sb("ids_all", [P, tiles, FIELDS], i32)
        idx = [sb(f"idx{s}", [P, FIELDS], i32) for s in range(PAIRED)]
        gath = [sb(f"gath{s}", [P, FIELDS, EMB]) for s in range(PAIRED)]
        emb_t = [sb(f"emb_t{s}", [P, EMB, 1 + FIELDS]) for s in range(PAIRED)]
        diag = [sb(f"diag{s}", [P, EMB, 1 + FIELDS, QUADS]) for s in range(PAIRED)]
        prod = [sb(f"prod_{c.name}", [P, EMB, c.pairs]) for c in CHUNKS]
        mom_all = sb("mom_all", [P, sum(c.others for c in CHUNKS) * rows])
        mom, at = [], 0
        for c in CHUNKS:
            mom.append(mom_all[:, at:at + c.others * rows].rearrange("p (j b) -> p j b", b=rows))
            at += c.others * rows
        fold_w = [sb(f"fold_w_{c.name}", [P, c.others, HC]) for c in CHUNKS]
        v = mom_all[:, 0:FIELDS * PAIRS].rearrange("p (j c) -> p j c", c=PAIRS)
        w1_sb = sb("w1_sb", [P, FIELDS, FIELDS])
        w1_pairs = sb("w1_pairs", [P, PAIRS])
        w2_sb = sb("w2_sb", [P, FIELDS, HC])
        b2_sb = sb("b2_sb", [P, 1])
        b2_k = sb("b2_k", [P, 1])
        ident = sb("ident", [P, P])
        wt1 = sb("wt1", [P, 2, m1 * P])
        wt1_dense = sb("wt1_dense", [n_dense, m1 * P])
        wt2 = sb("wt2", [P, m1, m2 * P])
        wt3 = sb("wt3", [P, m2])
        bt1 = sb("bt1", [P, m1])
        bt2 = sb("bt2", [P, m2])
        dense_sb = sb("dense_sb", [n_dense, rows])
        z_sb = sb("z_sb", [P, 2, rows])
        h1_sb = sb("h1_sb", [P, m1, rows])
        h2_sb = sb("h2_sb", [P, m2, rows])
        y_sb = sb("y_sb", [1, rows])

        bank = [ps(f"bank{i}", [P, 512]) for i in range(RING)]
        z_ps = ps("z_ps", [P, 2, rows])
        h1_ps = ps("h1_ps", [P, m1, rows])
        h2_ps = ps("h2_ps", [P, m2, rows])

        ids_loaded = sem("ids_loaded")
        w1_loaded = sem("w1_loaded")
        w2_loaded = sem("w2_loaded")
        mlp_loaded = sem("mlp_loaded")
        dense_loaded = sem("dense_loaded")
        consts_set = sem("consts_set")
        ident_zeroed = sem("ident_zeroed")
        ident_set = sem("ident_set")
        w1_diag_set = sem("w1_diag_set")
        w1_summed = sem("w1_summed")
        v_filled = sem("v_filled")
        v_copied = sem("v_copied")
        v_folded = sem("v_folded")
        wt_filled = sem("wt_filled")
        wt_copied = sem("wt_copied")
        b2_scaled = sem("b2_scaled")
        idx_staged = sem("idx_staged")
        tile_begun = sem("tile_begun")
        gathered = [sem(f"gathered{s}") for s in range(PAIRED)]
        transposed = sem("transposed")
        diag_ready = sem("diag_ready")
        prod_ready = [sem(f"prod_{c.name}_ready") for c in CHUNKS]
        bank_filled = sem("bank_filled")
        bank_emptied = sem("bank_emptied")
        z_filled = sem("z_filled")
        z_copied = sem("z_copied")
        h1_filled = sem("h1_filled")
        h1_ready = sem("h1_ready")
        h2_filled = sem("h2_filled")
        h2_ready = sem("h2_ready")
        y_filled = sem("y_filled")
        y_copied = sem("y_copied")
        y_stored = sem("y_stored")

        W1_LOADS, MLP_LOADS = 2, 6
        CONSTS = 2 * PAIRED + 1
        FOLDS = 2 * NX + (2 * NY - 1) + 2 * NX + NY + (2 * NZ - 1)

        turns = []
        for i, c in enumerate(CHUNKS):
            turns.append((i, 0, w1_pairs[:, c.first:c.first + c.pairs]))
            for j in range(c.others - 1):
                turns.append((i, 1 + j, v[:, j, c.first:c.first + c.pairs]))
        lots = []
        for i in range(3):
            mine = [t for t in turns if t[0] == i]
            lots += [mine[k:k + 4] for k in range(0, len(mine), 4)]

        block = ctx.enter_context(nc.Block())

        @block.sync
        def _(sp):
            sp.dma_start(ids_all[:, :, :], ids).then_inc(ids_loaded, 16)
            sp.dma_start(w1_sb[:, :, :], w1).then_inc(w1_loaded, 16)
            sp.dma_start(w1_pairs[:, COL_1:PAIRS], b1).then_inc(w1_loaded, 16)
            sp.dma_start(w2_sb[:, :, :], w2).then_inc(w2_loaded, 16)
            sp.dma_start(b2_sb[:, :], b2).then_inc(w2_loaded, 16)
            sp.dma_start(wt1[:, :, :], w_top1[0:2 * HC, :].rearrange("(k p) m -> p k m", p=P)).then_inc(mlp_loaded, 16)
            sp.dma_start(wt1_dense[:, :], w_top1[2 * HC:2 * HC + n_dense, :]).then_inc(mlp_loaded, 16)
            sp.dma_start(wt2[:, :, :], w_top2.rearrange("(k p) m -> p k m", p=P)).then_inc(mlp_loaded, 16)
            sp.dma_start(wt3[:, :], w_top3).then_inc(mlp_loaded, 16)
            sp.dma_start(bt1[:, :], b_top1).then_inc(mlp_loaded, 16)
            sp.dma_start(bt2[:, :], b_top2).then_inc(mlp_loaded, 16)

            def load_dense(n):
                sp.dma_start(dense_sb[:, :], dense_t[:, bass.ds(n * rows, rows)]).then_inc(dense_loaded, 16)

            def store_y(n):
                sp.wait_ge(y_copied, n + 1)
                sp.dma_start(y[:, bass.ds(n * rows, rows)], y_sb[:, :]).then_inc(y_stored, 16)

            load_dense(0)
            with sp.Fori(1, steps) as n:
                sp.wait_ge(h1_filled, m1 * n)
                load_dense(n)
                store_y(n - 1)
            store_y(steps - 1)
            sp.wait_ge(y_stored, 16 * steps)

        @block.gpsimd
        def _(pool):
            def gather(n, s, free):
                if free is not None:
                    pool.wait_ge(transposed, free)
                nc.gpsimd.tensor_copy(idx[s][:, :], ids_all[:, PAIRED * n + s, :]).then_inc(idx_staged, 1)
                pool.wait_ge(idx_staged, PAIRED * n + s + 1)
                pool.sem_inc(tile_begun, 1)
                for f in range(FIELDS):
                    nc.gpsimd.indirect_dma_start(
                        gath[s][:, f, :], None, tables[f],
                        bass.IndirectOffsetOnAxis(idx[s][:, f:f + 1], 0)).then_inc(gathered[s], 16)

            nc.gpsimd.memset(ident[:, :], 0.0).then_inc(ident_zeroed, 1)
            pool.wait_ge(ident_zeroed, 1)
            nc.gpsimd.affine_select(out=ident[:, :], in_=ident[:, :], compare_op=ALU.not_equal, fill=1.0, base=0,
                                    pattern=[[-1, P]], channel_multiplier=1).then_inc(ident_set, 1)
            pool.wait_ge(ids_loaded, 16)
            for s in range(PAIRED):
                gather(0, s, None)
            with pool.Fori(1, steps) as n:
                for s in range(PAIRED):
                    gather(n, s, PAIRED * n + s - 1)

        @block.scalar
        def _(act):
            act.wait_ge(w1_loaded, 16 * W1_LOADS)
            for first, size, field in ((COL_XX, NX, X0), (COL_YY, NY, Y0), (COL_ZZ, NZ, Z0)):
                for a in range(size):
                    col = first + tri_row(size, a)
                    last = nc.scalar.copy(w1_pairs[:, col:col + 1], w1_sb[:, field + a, field + a:field + a + 1])
            last.then_inc(w1_diag_set, 1)
            act.wait_ge(w2_loaded, 32)
            nc.scalar.mul(b2_k[:, :], b2_sb[:, :], float(EMB)).then_inc(b2_scaled, 1)
            for j in range(FIELDS):
                act.wait_ge(v_filled, j + 1)
                nc.scalar.copy(v[:, j, :], bank[j % RING][:, 0:PAIRS]).then_inc(v_copied, 1)
            for k, lot in enumerate(lots):
                act.wait_ge(wt_filled, k + 1)
                i, at, _ = lot[0]
                nc.scalar.copy(fold_w[i][0:CHUNKS[i].pairs, at:at + len(lot), :],
                               bank[k % RING][0:CHUNKS[i].pairs, 0:len(lot) * HC].rearrange(
                                   "p (j h) -> p j h", h=HC)).then_inc(wt_copied, 1)
            act.wait_ge(mlp_loaded, 16 * MLP_LOADS)
            act.wait_ge(b2_scaled, 1)

            def empty_banks(n, s, i):
                c = CHUNKS[i]
                for k in range(c.banks):
                    fill = FILLS * s + AFTER[i] - c.banks + k
                    act.wait_ge(bank_filled, FILLS * PAIRED * n + fill + 1)
                    groups = c.per_bank
                    at = s * P + k * groups * QUADS
                    src = bank[fill % RING][0:c.pairs, 0:groups * c.others * QUADS].rearrange(
                        "p (g j r) -> p j g r", g=groups, r=QUADS)
                    dst = mom[i][0:c.pairs, :, at:at + groups * QUADS].rearrange("p j (g r) -> p j g r", r=QUADS)
                    nc.scalar.copy(dst, src).then_inc(bank_emptied, 1)

            def relu_h1(n):
                for m in range(m1):
                    act.wait_ge(h1_filled, m1 * n + m // 2 * 2 + 2)
                    nc.scalar.activation(h1_sb[:, m, :], h1_ps[:, m, :], ACT.Relu,
                                         bias=bt1[:, m:m + 1]).then_inc(h1_ready, 1)

            def relu_h2(n):
                act.wait_ge(h2_filled, m2 * (n + 1))
                for m in range(m2):
                    nc.scalar.activation(h2_sb[:, m, :], h2_ps[:, m, :], ACT.Relu,
                                         bias=bt2[:, m:m + 1]).then_inc(h2_ready, 1)

            def copy_y(n, stored):
                act.wait_ge(y_filled, n + 1)
                if stored is not None:
                    act.wait_ge(y_stored, stored)
                nc.scalar.copy(y_sb[:, :], h2_ps[0:1, 0, :]).then_inc(y_copied, 1)

            def copy_z(n):
                act.wait_ge(z_filled, n + 1)
                nc.scalar.copy(z_sb[:, 0, :], z_ps[:, 0, :]).then_inc(z_copied, 1)
                nc.scalar.activation(z_sb[:, 1, :], z_ps[:, 1, :], ACT.Identity,
                                     bias=b2_k[:, :]).then_inc(z_copied, 1)

            for i in range(3):
                empty_banks(0, 0, i)
            for i in range(3):
                empty_banks(0, 1, i)
            copy_z(0)

            def step(n, stored):
                act.wait_ge(z_filled, n)
                for i in range(3):
                    empty_banks(n, 0, i)
                relu_h1(n - 1)
                empty_banks(n, 1, 0)
                relu_h2(n - 1)
                empty_banks(n, 1, 1)
                copy_y(n - 1, stored)
                empty_banks(n, 1, 2)
                copy_z(n)

            step(1, None)
            with act.Fori(2, steps) as n:
                step(n, 16 * (n - 1))
            relu_h1(steps - 1)
            relu_h2(steps - 1)
            copy_y(steps - 1, 16 * (steps - 1))

        @block.vector
        def _(dve):
            for s in range(PAIRED):
                nc.vector.memset(emb_t[s][:, :, 0:1], 1.0).then_inc(consts_set, 1)
                nc.vector.memset(diag[s][:, :, :, :], 0.0).then_inc(consts_set, 1)
            nc.vector.memset(prod[0][:, :, COL_1 - COL_ZZ:], 1.0).then_inc(consts_set, 1)

            dve.wait_ge(w1_loaded, 16 * W1_LOADS)
            for first, pf, pn, qf, qn in ((COL_XY, X0, NX, Y0, NY), (COL_XZ, X0, NX, Z0, NZ), (COL_YZ, Y0, NY, Z0, NZ)):
                nc.vector.tensor_tensor(
                    w1_pairs[:, first:first + pn * qn].rearrange("p (a b) -> p a b", b=qn),
                    w1_sb[:, pf:pf + pn, qf:qf + qn],
                    w1_sb[:, qf:qf + qn, pf:pf + pn].rearrange("p b a -> p a b"), ALU.add)
            for first, size, field in ((COL_XX, NX, X0), (COL_YY, NY, Y0), (COL_ZZ, NZ, Z0)):
                for a in range(size - 1):
                    col = first + tri_row(size, a) + 1
                    f = field + a
                    last = nc.vector.tensor_tensor(
                        w1_pairs[:, col:col + size - 1 - a], w1_sb[:, f, f + 1:field + size],
                        w1_sb[:, f + 1:field + size, f], ALU.add)
            last.then_inc(w1_summed, 1)

            def tile_in(n, s, diag_free):
                t = PAIRED * n + s
                dve.wait_ge(gathered[s], 16 * FIELDS * (n + 1))
                nc.vector.transpose(emb_t[s][:, :, 1:].rearrange("p c j -> p j c"),
                                    gath[s][:, :, :]).then_inc(transposed, 1)
                dve.wait_ge(transposed, t + 1)
                if diag_free is not None:
                    dve.wait_ge(bank_filled, diag_free)
                for r in range(QUADS):
                    q = slice(EMB * r, EMB * (r + 1))
                    nc.vector.tensor_copy(diag[s][q, :, :, r], emb_t[s][q, :, :]).then_inc(diag_ready, 1)

            def products(s, i, free):
                if free is not None:
                    dve.wait_ge(bank_filled, free)
                e = emb_t[s]
                c = CHUNKS[i]

                def rect(first, pf, pn, qf, qn):
                    at = first - c.first
                    return nc.vector.tensor_tensor(
                        prod[i][:, :, at:at + pn * qn].rearrange("p c (a b) -> p c a b", b=qn),
                        e[:, :, 1 + pf:1 + pf + pn].unsqueeze(3).broadcast_to([P, EMB, pn, qn]),
                        e[:, :, 1 + qf:1 + qf + qn].unsqueeze(2).broadcast_to([P, EMB, pn, qn]), ALU.mult)

                def upper(first, field, size):
                    for a in range(size):
                        at = first - c.first + tri_row(size, a)
                        f = 1 + field + a
                        last = nc.vector.tensor_tensor(
                            prod[i][:, :, at:at + size - a],
                            e[:, :, f:f + 1].broadcast_to([P, EMB, size - a]),
                            e[:, :, f:1 + field + size], ALU.mult)
                    return last

                if c.name == "a":
                    last = upper(COL_ZZ, Z0, NZ)
                elif c.name == "b":
                    rect(COL_YZ, Y0, NY, Z0, NZ)
                    last = upper(COL_YY, Y0, NY)
                else:
                    upper(COL_XX, X0, NX)
                    rect(COL_XY, X0, NX, Y0, NY)
                    last = rect(COL_XZ, X0, NX, Z0, NZ)
                last.then_inc(prod_ready[i], 1)

            def fold():
                done = [0]

                def add(out, in_):
                    nc.vector.tensor_tensor(out, out, in_, ALU.add).then_inc(v_folded, 1)
                    done[0] += 1
                    dve.wait_ge(v_folded, done[0])

                dve.wait_ge(v_copied, FIELDS)
                xy = v[:, :, COL_XY:COL_XZ].rearrange("p j (a b) -> p j a b", b=NY)
                xz = v[:, :, COL_XZ:COL_YZ].rearrange("p j (a b) -> p j a b", b=NZ)
                yz = v[:, :, COL_YZ:COL_YY].rearrange("p j (a b) -> p j a b", b=NZ)
                xyz = v[:, :, COL_XZ:COL_YY].rearrange("p j (a b) -> p j a b", b=NZ)
                for a in range(NX):
                    row = v[:, :, COL_XX + tri_row(NX, a):COL_XX + tri_row(NX, a) + NX - a].rearrange("p j b -> p b j")
                    add(xy[:, a, a:, :], row[:, :, Y0:Z0])
                    add(xz[:, a, a:, :], row[:, :, Z0:])
                for b in range(NY):
                    at = COL_YY + tri_row(NY, b)
                    add(v[:, 0:NX, at:at + NY - b], xy[:, Y0 + b:Z0, :, b].rearrange("p m a -> p a m"))
                    if b + 1 < NY:
                        add(v[:, 0:NX, at + 1:at + NY - b], xy[:, Y0 + b, :, b + 1:])
                for a in range(NX):
                    add(yz[:, a, :, :], xy[:, Z0:, a, :].rearrange("p m b -> p b m"))
                    add(yz[:, a, :, :], xz[:, Y0:Z0, a, :])
                for a in range(NY):
                    at = COL_YY + tri_row(NY, a)
                    add(yz[:, Y0 + a, a:, :], v[:, Z0:, at:at + NY - a].rearrange("p m b -> p b m"))
                for b in range(NZ):
                    at = COL_ZZ + tri_row(NZ, b)
                    add(v[:, 0:Z0, at:at + NZ - b], xyz[:, Z0 + b:, :, b].rearrange("p m a -> p a m"))
                    if b + 1 < NZ:
                        add(v[:, 0:Z0, at + 1:at + NZ - b], xyz[:, Z0 + b, :, b + 1:])
            dve.wait_ge(consts_set, CONSTS)
            fold()
            tile_in(0, 0, None)
            for i in range(3):
                products(0, i, None)
            tile_in(0, 1, None)
            for i in range(3):
                products(1, i, AFTER[i])

            with dve.Fori(1, steps) as n:
                for s in range(PAIRED):
                    before = FILLS * (PAIRED * n + s - 1)
                    tile_in(n, s, before)
                    for i in range(3):
                        products(s, i, before + AFTER[i])

        @block.tensor
        def _(pe):
            pe.wait_ge(w2_loaded, 32)
            pe.wait_ge(w1_diag_set, 1)
            pe.wait_ge(w1_summed, 1)
            for j in range(FIELDS):
                if j >= RING:
                    pe.wait_ge(v_copied, j - RING + 1)
                nc.tensor.matmul(bank[j % RING][:, 0:PAIRS], w2_sb[:, j, :], w1_pairs[:, :],
                                 start=True, stop=True).then_inc(v_filled, 1)
            pe.wait_ge(v_folded, FOLDS)
            pe.wait_ge(ident_set, 1)
            for k, lot in enumerate(lots):
                if k >= RING:
                    pe.wait_ge(wt_copied, k - RING + 1)
                for g, (i, _, src) in enumerate(lot):
                    last = nc.tensor.transpose(bank[k % RING][0:CHUNKS[i].pairs, g * HC:(g + 1) * HC], src, ident[:, :])
                last.then_inc(wt_filled, 1)
            pe.wait_ge(wt_copied, len(lots))
            pe.wait_ge(mlp_loaded, 16 * MLP_LOADS)

            def moments(n, s, i, first):
                c = CHUNKS[i]
                if i == 0:
                    pe.wait_ge(diag_ready, QUADS * (PAIRED * n + s + 1))
                pe.wait_ge(prod_ready[i], PAIRED * n + s + 1)
                for k in range(c.banks):
                    fill = FILLS * s + AFTER[i] - c.banks + k
                    if not (first and fill < RING):
                        pe.wait_ge(bank_emptied, FILLS * PAIRED * n + fill - RING + 1)
                    for g in range(c.per_bank):
                        at = g * c.others * QUADS
                        last = nc.tensor.matmul(bank[fill % RING][0:c.pairs, at:at + c.others * QUADS],
                                                prod[i][:, k * c.per_bank + g, :],
                                                diag[s][:, k * c.per_bank + g, 0:c.others, :],
                                                start=True, stop=True)
                    last.then_inc(bank_filled, 1)

            def contract(n, first):
                if not first:
                    pe.wait_ge(z_copied, 2 * n)
                for i, c in enumerate(CHUNKS):
                    pe.wait_ge(bank_emptied, FILLS * (PAIRED * n + 1) + AFTER[i])
                    for j in range(1, c.others):
                        nc.tensor.matmul(z_ps[:, 1, :], fold_w[i][0:c.pairs, j, :], mom[i][0:c.pairs, j, :],
                                         start=(i == 0 and j == 1), stop=(i == 2 and j == c.others - 1))
                for i, c in enumerate(CHUNKS):
                    last = nc.tensor.matmul(z_ps[:, 0, :], fold_w[i][0:c.pairs, 0, :], mom[i][0:c.pairs, 0, :],
                                            start=(i == 0), stop=(i == 2))
                last.then_inc(z_filled, 1)

            def layer1(n):
                pe.wait_ge(z_copied, 2 * (n + 1))
                pe.wait_ge(dense_loaded, 16 * (n + 1))
                for m in range(m1):
                    cols = slice(m * P, (m + 1) * P)
                    for k in range(2):
                        nc.tensor.matmul(h1_ps[:, m, :], wt1[:, k, cols], z_sb[:, k, :], start=(k == 0), stop=False)
                    nc.tensor.matmul(h1_ps[:, m, :], wt1_dense[:, cols], dense_sb[:, :],
                                     start=False, stop=True).then_inc(h1_filled, 1)

            def layer2(n, first):
                pe.wait_ge(h1_ready, m1 * (n + 1))
                if not first:
                    pe.wait_ge(y_copied, n)
                for m in range(m2):
                    for k in range(m1):
                        last = nc.tensor.matmul(h2_ps[:, m, :], wt2[:, k, m * P:(m + 1) * P], h1_sb[:, k, :],
                                                start=(k == 0), stop=(k == m1 - 1))
                    last.then_inc(h2_filled, 1)

            def layer3(n):
                pe.wait_ge(h2_ready, m2 * (n + 1))
                for k in range(m2):
                    last = nc.tensor.matmul(h2_ps[0:1, 0, :], wt3[:, k:k + 1], h2_sb[:, k, :],
                                            start=(k == 0), stop=(k == m2 - 1))
                last.then_inc(y_filled, 1)

            for s in range(PAIRED):
                for i in range(3):
                    moments(0, s, i, s == 0)
            contract(0, True)

            def step(n, first):
                for i in range(3):
                    moments(n, 0, i, False)
                layer1(n - 1)
                moments(n, 1, 0, False)
                layer2(n - 1, first)
                moments(n, 1, 1, False)
                layer3(n - 1)
                moments(n, 1, 2, False)
                contract(n, False)

            step(1, True)
            with pe.Fori(2, steps) as n:
                step(n, False)
            layer1(steps - 1)
            layer2(steps - 1, False)
            layer3(steps - 1)


def kernel(**inputs):
    import numpy as np
    import concourse.bacc as bacc
    from concourse.bass_utils import run_bass_kernel_spmd

    nc = bacc.Bacc("TRN2", target_bir_lowering=False, num_devices=1)
    a = {k: np.asarray(x) for k, x in inputs.items()}
    batch = a["ids"].shape[0]
    ids = a["ids"].reshape(batch // P, EMB, QUADS, FIELDS).transpose(2, 1, 0, 3).reshape(P, batch // P, FIELDS)
    arrays = {"dense_t": a["dense_ctx"].T, "ids": ids}
    for f in range(FIELDS):
        arrays[f"tbl_{f}"] = a[f"tbl_{f}"]
    arrays["w_top1"] = a["W_top1"]
    arrays["b_top1"] = a["b_top1"].reshape(-1, P).T
    arrays["w_top2"] = a["W_top2"]
    arrays["b_top2"] = a["b_top2"].reshape(-1, P).T
    arrays["w_top3"] = a["W_top3"].reshape(-1, P).T
    arrays["w1"] = a["L0_rec_W1"]
    arrays["b1"] = a["L0_rec_b1"].reshape(HC, 1)
    arrays["w2"] = a["L0_rec_W2"].transpose(1, 2, 0)
    arrays["b2"] = a["L0_rec_b2"].reshape(HC, 1)
    arrays = {f"in_{k}": np.ascontiguousarray(x) for k, x in arrays.items()}
    ap = {k[3:]: nc.dram_tensor(k, x.shape, mybir.dt.from_np(x.dtype), kind="ExternalInput").ap()
          for k, x in arrays.items()}
    y = nc.dram_tensor("y", (1, batch), mybir.dt.float32, kind="ExternalOutput").ap()
    dlrm_tower(nc, ap["dense_t"], ap["ids"], [ap[f"tbl_{f}"] for f in range(FIELDS)], ap["w_top1"], ap["b_top1"],
               ap["w_top2"], ap["b_top2"], ap["w_top3"], ap["w1"], ap["b1"], ap["w2"], ap["b2"], y)
    r = run_bass_kernel_spmd(nc, [arrays], core_ids=[0])
    return r.results[0]["y"].reshape(batch, 1)
```

```python
import concourse.bass as bass
from concourse import mybir
from contextlib import ExitStack

FIELDS = 26
EMB = 32
HC = 128
P = 128
QUADS = P // EMB
PAIRED = 2
RING = 4
HALF = FIELDS // 2
B1, B2 = 7, HALF - 7
VARS = FIELDS + 1
ONE = HALF
VW0 = HALF + 1


def tri(n):
    return n * (n + 1) // 2


def tri_row(n, a):
    return a * n - a * (a - 1) // 2


U_T1 = 0
U_T2 = U_T1 + tri(B1)
U_11 = U_T2 + tri(B2)
U_X = U_11 + 1
U_1U = U_X + B1 * B2
U_ROWS = U_1U + HALF
W_X = 0
W_GAP = W_X + B1 * B2
W_T1 = 64
W_T2 = W_T1 + tri(B1)
W_ROWS = W_T2 + tri(B2)
COL_W = U_ROWS
COL_X = COL_W + W_ROWS
COLS = COL_X + HALF * HALF
X_PER = P // HALF
KINDS = {"u": (U_ROWS, 0, 1 + HALF), "w": (W_ROWS, 1 + HALF, 1 + HALF), "i": (W_ROWS, 2 + 2 * HALF, HALF),
         "x0": (X_PER * HALF, 2 + 3 * HALF, 1), "x1": ((HALF - X_PER) * HALF, 3 + 3 * HALF, 1)}
M_TILES = 4 + 3 * HALF
PER_BANK = 512 // (VARS * QUADS)
BANKS = EMB // PER_BANK
FILLS = 2 * BANKS


def dlrm_tower(nc, dense_t, ids, tables, w_top1, b_top1, w_top2, b_top2, w_top3, w1, b1, w2, b2, y):
    fp32 = mybir.dt.float32
    i32 = mybir.dt.int32
    ALU = mybir.AluOpType
    ACT = mybir.ActivationFunctionType

    batch = dense_t.shape[1]
    n_dense = dense_t.shape[0]
    tiles = batch // P
    steps = tiles // PAIRED
    rows = PAIRED * P
    m1 = w_top1.shape[1] // P
    m2 = w_top2.shape[1] // P
    assert FILLS * PAIRED % RING == 0 and 2 * HC + n_dense == w_top1.shape[0] and m1 % 2 == 0
    assert M_TILES * rows >= FIELDS * COLS and COLS <= 512

    ctx = ExitStack()
    with ctx:
        def sb(name, shape, dt=fp32):
            return ctx.enter_context(nc.sbuf_tensor(name, shape, dt))

        def ps(name, shape):
            return ctx.enter_context(nc.psum_tensor(name, shape, fp32))

        def sem(name):
            return ctx.enter_context(nc.semaphore(name))

        ids_all = sb("ids_all", [P, tiles, FIELDS], i32)
        idx = [sb(f"idx{s}", [P, FIELDS], i32) for s in range(PAIRED)]
        gath = [sb(f"gath{s}", [P, FIELDS, EMB]) for s in range(PAIRED)]
        emb_t = [sb(f"emb_t{s}", [P, EMB, VARS]) for s in range(PAIRED)]
        diag = [sb(f"diag{s}", [P, EMB, VARS, QUADS]) for s in range(PAIRED)]
        prod = [[sb(f"prod_u{s}", [P, EMB, U_ROWS]), sb(f"prod_w{s}", [P, EMB, W_ROWS])] for s in range(PAIRED)]
        mom = sb("mom", [P, M_TILES, rows])
        fold_w = sb("fold_w", [P, M_TILES, HC])
        v = mom[:, :, :].rearrange("p j b -> p (j b)")[:, 0:FIELDS * COLS].rearrange("p (j c) -> p j c", c=COLS)
        w1_sb = sb("w1_sb", [P, FIELDS, FIELDS])
        w1_pairs = sb("w1_pairs", [P, COLS])
        w2_sb = sb("w2_sb", [P, FIELDS, HC])
        b2_sb = sb("b2_sb", [P, 1])
        b2_k = sb("b2_k", [P, 1])
        ident = sb("ident", [P, P])
        wt1 = sb("wt1", [P, 2, m1 * P])
        wt1_dense = sb("wt1_dense", [n_dense, m1 * P])
        wt2 = sb("wt2", [P, m1, m2 * P])
        wt3 = sb("wt3", [P, m2])
        bt1 = sb("bt1", [P, m1])
        bt2 = sb("bt2", [P, m2])
        dense_sb = sb("dense_sb", [n_dense, rows])
        z_sb = sb("z_sb", [P, 2, rows])
        h1_sb = sb("h1_sb", [P, m1, rows])
        h2_sb = sb("h2_sb", [P, m2, rows])
        y_sb = sb("y_sb", [1, rows])

        bank = [ps(f"bank{i}", [P, 512]) for i in range(RING)]
        z_ps = ps("z_ps", [P, 2, rows])
        h1_ps = ps("h1_ps", [P, m1, rows])
        h2_ps = ps("h2_ps", [P, m2, rows])

        ids_loaded = sem("ids_loaded")
        w1_loaded = sem("w1_loaded")
        w2_loaded = sem("w2_loaded")
        mlp_loaded = sem("mlp_loaded")
        dense_loaded = sem("dense_loaded")
        consts_set = sem("consts_set")
        ident_zeroed = sem("ident_zeroed")
        ident_set = sem("ident_set")
        w1_diag_set = sem("w1_diag_set")
        w1_summed = sem("w1_summed")
        v_filled = sem("v_filled")
        v_copied = sem("v_copied")
        v_added = sem("v_added")
        v_folded = sem("v_folded")
        wt_filled = sem("wt_filled")
        wt_copied = sem("wt_copied")
        b2_scaled = sem("b2_scaled")
        idx_staged = sem("idx_staged")
        tile_begun = sem("tile_begun")
        gathered = [sem(f"gathered{s}") for s in range(PAIRED)]
        transposed = sem("transposed")
        diag_ready = sem("diag_ready")
        prod_ready = [sem("prod_u_ready"), sem("prod_w_ready")]
        bank_filled = sem("bank_filled")
        bank_emptied = sem("bank_emptied")
        cross_moved = sem("cross_moved")
        z_filled = sem("z_filled")
        z_copied = sem("z_copied")
        h1_filled = sem("h1_filled")
        h1_ready = sem("h1_ready")
        h2_filled = sem("h2_filled")
        h2_ready = sem("h2_ready")
        y_filled = sem("y_filled")
        y_copied = sem("y_copied")
        y_stored = sem("y_stored")

        W1_LOADS, MLP_LOADS = 2, 6
        CONSTS = 4 * PAIRED
        PARTS = 2

        turns = {
            "u": [w1_pairs[:, 0:U_ROWS]] + [v[:, HALF + w, 0:U_ROWS] for w in range(HALF)],
            "w": [v[:, u, COL_W:COL_X] for u in range(HALF)] + [w1_pairs[:, COL_W:COL_X]],
            "i": [v[:, i, COL_X:COL_X + W_ROWS] for i in range(HALF)],
            "x0": [w1_pairs[:, COL_X:COL_X + X_PER * HALF]],
            "x1": [w1_pairs[:, COL_X + X_PER * HALF:COLS]],
        }
        lots = []
        for kind, sources in turns.items():
            size, first, _ = KINDS[kind]
            lots += [(size, first + k, sources[k:k + 4]) for k in range(0, len(sources), 4)]

        TRIANGLES = ((U_T1, B1, 0), (U_T2, B2, B1), (COL_W + W_T1, B1, HALF), (COL_W + W_T2, B2, HALF + B1))

        block = ctx.enter_context(nc.Block())

        @block.sync
        def _(sp):
            sp.dma_start(ids_all[:, :, :], ids).then_inc(ids_loaded, 16)
            sp.dma_start(w1_sb[:, :, :], w1).then_inc(w1_loaded, 16)
            sp.dma_start(w1_pairs[:, U_11:U_11 + 1], b1).then_inc(w1_loaded, 16)
            sp.dma_start(w2_sb[:, :, :], w2).then_inc(w2_loaded, 16)
            sp.dma_start(b2_sb[:, :], b2).then_inc(w2_loaded, 16)
            sp.dma_start(wt1[:, :, :], w_top1[0:2 * HC, :].rearrange("(k p) m -> p k m", p=P)).then_inc(mlp_loaded, 16)
            sp.dma_start(wt1_dense[:, :], w_top1[2 * HC:2 * HC + n_dense, :]).then_inc(mlp_loaded, 16)
            sp.dma_start(wt2[:, :, :], w_top2.rearrange("(k p) m -> p k m", p=P)).then_inc(mlp_loaded, 16)
            sp.dma_start(wt3[:, :], w_top3).then_inc(mlp_loaded, 16)
            sp.dma_start(bt1[:, :], b_top1).then_inc(mlp_loaded, 16)
            sp.dma_start(bt2[:, :], b_top2).then_inc(mlp_loaded, 16)

            def load_dense(n):
                sp.dma_start(dense_sb[:, :], dense_t[:, bass.ds(n * rows, rows)]).then_inc(dense_loaded, 16)

            def store_y(n):
                sp.wait_ge(y_copied, n + 1)
                sp.dma_start(y[:, bass.ds(n * rows, rows)], y_sb[:, :]).then_inc(y_stored, 16)

            def move_cross(n):
                sp.wait_ge(bank_emptied, PARTS * (FILLS * (PAIRED * n + 1) + BANKS))
                for w in range(HALF):
                    kind, at = ("x0", w) if w < X_PER else ("x1", w - X_PER)
                    sp.dma_start(mom[at * HALF:(at + 1) * HALF, KINDS[kind][1], :],
                                 mom[U_1U:U_ROWS, KINDS["u"][1] + 1 + w, :]).then_inc(cross_moved, 16)

            load_dense(0)
            move_cross(0)
            with sp.Fori(1, steps) as n:
                sp.wait_ge(h1_filled, m1 * n)
                load_dense(n)
                store_y(n - 1)
                move_cross(n)
            store_y(steps - 1)
            sp.wait_ge(y_stored, 16 * steps)

        @block.gpsimd
        def _(pool):
            def gather(n, s, free):
                if free is not None:
                    pool.wait_ge(transposed, free)
                nc.gpsimd.tensor_copy(idx[s][:, :], ids_all[:, PAIRED * n + s, :]).then_inc(idx_staged, 1)
                pool.wait_ge(idx_staged, PAIRED * n + s + 1)
                pool.sem_inc(tile_begun, 1)
                for f in range(FIELDS):
                    nc.gpsimd.indirect_dma_start(
                        gath[s][:, f, :], None, tables[f],
                        bass.IndirectOffsetOnAxis(idx[s][:, f:f + 1], 0)).then_inc(gathered[s], 16)

            nc.gpsimd.memset(ident[:, :], 0.0).then_inc(ident_zeroed, 1)
            pool.wait_ge(ident_zeroed, 1)
            nc.gpsimd.affine_select(out=ident[:, :], in_=ident[:, :], compare_op=ALU.not_equal, fill=1.0, base=0,
                                    pattern=[[-1, P]], channel_multiplier=1).then_inc(ident_set, 1)
            pool.wait_ge(ids_loaded, 16)
            for s in range(PAIRED):
                gather(0, s, None)
            with pool.Fori(1, steps) as n:
                for s in range(PAIRED):
                    gather(n, s, 2 * (PAIRED * n + s - 1))

        @block.scalar
        def _(act):
            act.wait_ge(w1_loaded, 16 * W1_LOADS)
            for first, size, field in TRIANGLES:
                for a in range(size):
                    col = first + tri_row(size, a)
                    last = nc.scalar.copy(w1_pairs[:, col:col + 1], w1_sb[:, field + a, field + a:field + a + 1])
            last.then_inc(w1_diag_set, 1)
            act.wait_ge(w2_loaded, 32)
            nc.scalar.mul(b2_k[:, :], b2_sb[:, :], float(EMB)).then_inc(b2_scaled, 1)
            for j in range(FIELDS):
                act.wait_ge(v_filled, j + 1)
                nc.scalar.copy(v[:, j, :], bank[j % RING][:, 0:COLS]).then_inc(v_copied, 1)
            for k, (size, at, sources) in enumerate(lots):
                act.wait_ge(wt_filled, k + 1)
                nc.scalar.copy(fold_w[0:size, at:at + len(sources), :],
                               bank[k % RING][0:size, 0:len(sources) * HC].rearrange(
                                   "p (j h) -> p j h", h=HC)).then_inc(wt_copied, 1)
            act.wait_ge(mlp_loaded, 16 * MLP_LOADS)
            act.wait_ge(b2_scaled, 1)

            def empty_banks(n, s, i):
                for k in range(BANKS):
                    fill = FILLS * s + BANKS * i + k
                    act.wait_ge(bank_filled, FILLS * PAIRED * n + fill + 1)
                    at = s * P + k * PER_BANK * QUADS
                    src = bank[fill % RING][:, 0:PER_BANK * VARS * QUADS].rearrange(
                        "p (g j r) -> p j g r", j=VARS, r=QUADS)
                    dst = mom[:, :, at:at + PER_BANK * QUADS].rearrange("p j (g r) -> p j g r", r=QUADS)
                    size, first, count = KINDS["w" if i else "u"]
                    own = slice(0, ONE + 1) if i else slice(ONE, VARS)
                    inner = slice(VW0, VARS) if i else slice(0, ONE)
                    part = slice(W_T1, W_ROWS) if i else slice(0, W_T1)
                    _, first_i, count_i = KINDS["i"]
                    nc.scalar.copy(dst[0:size, first:first + count], src[0:size, own]).then_inc(bank_emptied, 1)
                    nc.scalar.copy(dst[part, first_i:first_i + count_i], src[part, inner]).then_inc(bank_emptied, 1)

            def relu_h1(n):
                for m in range(m1):
                    act.wait_ge(h1_filled, m1 * n + m // 2 * 2 + 2)
                    nc.scalar.activation(h1_sb[:, m, :], h1_ps[:, m, :], ACT.Relu,
                                         bias=bt1[:, m:m + 1]).then_inc(h1_ready, 1)

            def relu_h2(n):
                act.wait_ge(h2_filled, m2 * (n + 1))
                for m in range(m2):
                    nc.scalar.activation(h2_sb[:, m, :], h2_ps[:, m, :], ACT.Relu,
                                         bias=bt2[:, m:m + 1]).then_inc(h2_ready, 1)

            def copy_y(n, stored):
                act.wait_ge(y_filled, n + 1)
                if stored is not None:
                    act.wait_ge(y_stored, stored)
                nc.scalar.copy(y_sb[:, :], h2_ps[0:1, 0, :]).then_inc(y_copied, 1)

            def copy_z(n):
                act.wait_ge(z_filled, n + 1)
                nc.scalar.copy(z_sb[:, 0, :], z_ps[:, 0, :]).then_inc(z_copied, 1)
                nc.scalar.activation(z_sb[:, 1, :], z_ps[:, 1, :], ACT.Identity,
                                     bias=b2_k[:, :]).then_inc(z_copied, 1)

            for s in range(PAIRED):
                for i in range(2):
                    empty_banks(0, s, i)
            copy_z(0)

            def step(n, stored):
                act.wait_ge(z_filled, n)
                empty_banks(n, 0, 0)
                relu_h1(n - 1)
                empty_banks(n, 0, 1)
                relu_h2(n - 1)
                empty_banks(n, 1, 0)
                copy_y(n - 1, stored)
                empty_banks(n, 1, 1)
                copy_z(n)

            step(1, None)
            with act.Fori(2, steps) as n:
                step(n, 16 * (n - 1))
            relu_h1(steps - 1)
            relu_h2(steps - 1)
            copy_y(steps - 1, 16 * (steps - 1))

        @block.vector
        def _(dve):
            for s in range(PAIRED):
                nc.vector.memset(emb_t[s][:, :, ONE:VW0], 1.0).then_inc(consts_set, 1)
                nc.vector.memset(diag[s][:, :, :, :], 0.0).then_inc(consts_set, 1)
                nc.vector.memset(prod[s][0][:, :, U_11:U_X], 1.0).then_inc(consts_set, 1)
                nc.vector.memset(prod[s][1][:, :, W_GAP:W_T1], 0.0).then_inc(consts_set, 1)
            nc.vector.memset(w1_pairs[:, U_1U:U_ROWS], 0.0)
            nc.vector.memset(w1_pairs[:, COL_W + W_GAP:COL_W + W_T1], 0.0)

            dve.wait_ge(w1_loaded, 16 * W1_LOADS)
            for first, pf in ((U_X, 0), (COL_W + W_X, HALF)):
                qf = pf + B1
                nc.vector.tensor_tensor(
                    w1_pairs[:, first:first + B1 * B2].rearrange("p (a b) -> p a b", b=B2),
                    w1_sb[:, pf:qf, qf:qf + B2],
                    w1_sb[:, qf:qf + B2, pf:qf].rearrange("p b a -> p a b"), ALU.add)
            nc.vector.tensor_tensor(
                w1_pairs[:, COL_X:].rearrange("p (w u) -> p w u", u=HALF), w1_sb[:, HALF:, 0:HALF],
                w1_sb[:, 0:HALF, HALF:].rearrange("p u w -> p w u"), ALU.add)
            for first, size, field in TRIANGLES:
                for a in range(size - 1):
                    col = first + tri_row(size, a) + 1
                    f = field + a
                    last = nc.vector.tensor_tensor(
                        w1_pairs[:, col:col + size - 1 - a], w1_sb[:, f, f + 1:field + size],
                        w1_sb[:, f + 1:field + size, f], ALU.add)
            last.then_inc(w1_summed, 1)

            def fold():
                cross = v[:, :, COL_X:].rearrange("p j (w u) -> p j w u", u=HALF)
                x_u = v[:, :, U_X:U_1U].rearrange("p j (a b) -> p j a b", b=B2)
                x_w = v[:, :, COL_W + W_X:COL_W + W_GAP].rearrange("p j (a b) -> p j a b", b=B2)
                first, second = [], []
                for t1, t2, f, x, across in ((U_T1, U_T2, 0, x_u, cross),
                                             (COL_W + W_T1, COL_W + W_T2, HALF, x_w,
                                              cross.rearrange("p j w u -> p j u w"))):
                    g = HALF - f
                    others = slice(g, g + HALF)
                    for t, n, lo in ((t1, B1, 0), (t2, B2, B1)):
                        for a in range(n):
                            at = t + tri_row(n, a)
                            first.append((v[:, others, at:at + n - a], across[:, f + lo + a, :, lo + a:lo + n]))
                            if a + 1 < n:
                                second.append((v[:, others, at + 1:at + n - a],
                                               across[:, f + lo + a + 1:f + lo + n, :, lo + a].rearrange(
                                                   "p b o -> p o b")))
                    first.append((x[:, others, :, :], across[:, f + B1:f + HALF, :, 0:B1].rearrange(
                        "p b o a -> p o a b")))
                    second.append((x[:, others, :, :], across[:, f:f + B1, :, B1:HALF].rearrange(
                        "p a o b -> p o a b")))
                    for a in range(B1):
                        at = t1 + tri_row(B1, a)
                        outer = slice(f + B1, f + HALF)
                        first.append((v[:, outer, at:at + B1 - a],
                                      x[:, f + a:f + B1, a, :].rearrange("p m b -> p b m")))
                        if a + 1 < B1:
                            second.append((v[:, outer, at + 1:at + B1 - a],
                                           x[:, f + a, a + 1:, :].rearrange("p m b -> p b m")))
                    for b in range(B2):
                        at = t2 + tri_row(B2, b)
                        outer = slice(f, f + B1)
                        first.append((v[:, outer, at:at + B2 - b],
                                      x[:, f + B1 + b:f + HALF, :, b].rearrange("p m a -> p a m")))
                        if b + 1 < B2:
                            second.append((v[:, outer, at + 1:at + B2 - b], x[:, f + B1 + b, :, b + 1:]))
                dve.wait_ge(v_copied, FIELDS)
                for kept, left in first:
                    last = nc.vector.tensor_tensor(kept, kept, left, ALU.add)
                last.then_inc(v_added, 1)
                dve.wait_ge(v_added, 1)
                for kept, left in second:
                    last = nc.vector.tensor_tensor(kept, kept, left, ALU.add)
                last.then_inc(v_added, 1)
                dve.wait_ge(v_added, 2)
                inner = v[:, 0:HALF, COL_X:COL_X + W_ROWS]
                nc.vector.tensor_copy(inner[:, :, 0:U_X], v[:, 0:HALF, 0:U_X])
                nc.vector.memset(inner[:, :, U_X:W_T1], 0.0)
                nc.vector.tensor_copy(inner[:, :, W_T1:], v[:, HALF:, COL_W + W_T1:COL_X]).then_inc(v_folded, 1)

            def tile_in(n, s, free):
                t = PAIRED * n + s
                dve.wait_ge(gathered[s], 16 * FIELDS * (n + 1))
                for field, at in ((0, 0), (HALF, VW0)):
                    nc.vector.transpose(emb_t[s][:, :, at:at + HALF].rearrange("p c j -> p j c"),
                                        gath[s][:, field:field + HALF, :]).then_inc(transposed, 1)
                dve.wait_ge(transposed, 2 * (t + 1))
                if free is not None:
                    dve.wait_ge(bank_filled, free)
                for r in range(QUADS):
                    q = slice(EMB * r, EMB * (r + 1))
                    nc.vector.tensor_copy(diag[s][q, :, :, r], emb_t[s][q, :, :]).then_inc(diag_ready, 1)

            def products(s):
                e = emb_t[s]
                for i, (t1, t2, x, at) in enumerate(((U_T1, U_T2, U_X, 0), (W_T1, W_T2, W_X, VW0))):
                    out = prod[s][i]
                    for t, n, lo in ((t1, B1, at), (t2, B2, at + B1)):
                        for a in range(n):
                            col = t + tri_row(n, a)
                            nc.vector.tensor_tensor(
                                out[:, :, col:col + n - a], e[:, :, lo + a:lo + a + 1].broadcast_to([P, EMB, n - a]),
                                e[:, :, lo + a:lo + n], ALU.mult)
                    last = nc.vector.tensor_tensor(
                        out[:, :, x:x + B1 * B2].rearrange("p c (a b) -> p c a b", b=B2),
                        e[:, :, at:at + B1].unsqueeze(3).broadcast_to([P, EMB, B1, B2]),
                        e[:, :, at + B1:at + HALF].unsqueeze(2).broadcast_to([P, EMB, B1, B2]), ALU.mult)
                    if i == 0:
                        last = nc.vector.tensor_copy(out[:, :, U_1U:U_ROWS], e[:, :, 0:HALF])
                    last.then_inc(prod_ready[i], 1)

            dve.wait_ge(consts_set, CONSTS)
            fold()
            for s in range(PAIRED):
                tile_in(0, s, None)
                products(s)
            with dve.Fori(1, steps) as n:
                for s in range(PAIRED):
                    tile_in(n, s, FILLS * (PAIRED * n + s - 1))
                    products(s)

        @block.tensor
        def _(pe):
            pe.wait_ge(w2_loaded, 32)
            pe.wait_ge(w1_diag_set, 1)
            pe.wait_ge(w1_summed, 1)
            for j in range(FIELDS):
                if j >= RING:
                    pe.wait_ge(v_copied, j - RING + 1)
                nc.tensor.matmul(bank[j % RING][:, 0:COLS], w2_sb[:, j, :], w1_pairs[:, :],
                                 start=True, stop=True).then_inc(v_filled, 1)
            pe.wait_ge(v_folded, 1)
            pe.wait_ge(ident_set, 1)
            for k, (size, _, sources) in enumerate(lots):
                if k >= RING:
                    pe.wait_ge(wt_copied, k - RING + 1)
                for g, src in enumerate(sources):
                    last = nc.tensor.transpose(bank[k % RING][0:size, g * HC:(g + 1) * HC], src, ident[:, :])
                last.then_inc(wt_filled, 1)
            pe.wait_ge(wt_copied, len(lots))
            pe.wait_ge(mlp_loaded, 16 * MLP_LOADS)

            def moments(n, s, i, first):
                size = W_ROWS if i else U_ROWS
                if i == 0:
                    pe.wait_ge(diag_ready, QUADS * (PAIRED * n + s + 1))
                pe.wait_ge(prod_ready[i], PAIRED * n + s + 1)
                for k in range(BANKS):
                    fill = FILLS * s + BANKS * i + k
                    if not (first and fill < RING):
                        pe.wait_ge(bank_emptied, PARTS * (FILLS * PAIRED * n + fill - RING + 1))
                    for g in range(PER_BANK):
                        at = g * VARS * QUADS
                        last = nc.tensor.matmul(bank[fill % RING][0:size, at:at + VARS * QUADS],
                                                prod[s][i][:, k * PER_BANK + g, :],
                                                diag[s][:, k * PER_BANK + g, :, :], start=True, stop=True)
                    last.then_inc(bank_filled, 1)

            def contract(n, first):
                if not first:
                    pe.wait_ge(z_copied, 2 * n)
                done = FILLS * (PAIRED * n + 1)
                quadratic = [("u", 0), ("w", HALF), ("x0", 0), ("x1", 0)]
                cubic = [("u", 1 + w) for w in range(HALF)] + [("w", u) for u in range(HALF)] \
                    + [("i", f) for f in range(HALF)]
                for z, terms in ((1, cubic), (0, quadratic)):
                    for k, (kind, j) in enumerate(terms):
                        if z == 1 and k == 0:
                            pe.wait_ge(bank_emptied, PARTS * (done + BANKS))
                        if z == 1 and k == HALF:
                            pe.wait_ge(bank_emptied, PARTS * (done + FILLS))
                        if kind == "x0":
                            pe.wait_ge(cross_moved, 16 * HALF * (n + 1))
                        size, at, _ = KINDS[kind]
                        last = nc.tensor.matmul(z_ps[:, z, :], fold_w[0:size, at + j, :], mom[0:size, at + j, :],
                                                start=(k == 0), stop=(k == len(terms) - 1))
                last.then_inc(z_filled, 1)

            def layer1(n):
                pe.wait_ge(z_copied, 2 * (n + 1))
                pe.wait_ge(dense_loaded, 16 * (n + 1))
                for m in range(m1):
                    cols = slice(m * P, (m + 1) * P)
                    for k in range(2):
                        nc.tensor.matmul(h1_ps[:, m, :], wt1[:, k, cols], z_sb[:, k, :], start=(k == 0), stop=False)
                    nc.tensor.matmul(h1_ps[:, m, :], wt1_dense[:, cols], dense_sb[:, :],
                                     start=False, stop=True).then_inc(h1_filled, 1)

            def layer2(n, first):
                pe.wait_ge(h1_ready, m1 * (n + 1))
                if not first:
                    pe.wait_ge(y_copied, n)
                for m in range(m2):
                    for k in range(m1):
                        last = nc.tensor.matmul(h2_ps[:, m, :], wt2[:, k, m * P:(m + 1) * P], h1_sb[:, k, :],
                                                start=(k == 0), stop=(k == m1 - 1))
                    last.then_inc(h2_filled, 1)

            def layer3(n):
                pe.wait_ge(h2_ready, m2 * (n + 1))
                for k in range(m2):
                    last = nc.tensor.matmul(h2_ps[0:1, 0, :], wt3[:, k:k + 1], h2_sb[:, k, :],
                                            start=(k == 0), stop=(k == m2 - 1))
                last.then_inc(y_filled, 1)

            for s in range(PAIRED):
                for i in range(2):
                    moments(0, s, i, s == 0)
            contract(0, True)

            def step(n, first):
                moments(n, 0, 0, False)
                layer1(n - 1)
                moments(n, 0, 1, False)
                layer2(n - 1, first)
                moments(n, 1, 0, False)
                layer3(n - 1)
                moments(n, 1, 1, False)
                contract(n, False)

            step(1, True)
            with pe.Fori(2, steps) as n:
                step(n, False)
            layer1(steps - 1)
            layer2(steps - 1, False)
            layer3(steps - 1)


def kernel(**inputs):
    import numpy as np
    import concourse.bacc as bacc
    from concourse.bass_utils import run_bass_kernel_spmd

    nc = bacc.Bacc("TRN2", target_bir_lowering=False, num_devices=1)
    a = {k: np.asarray(x) for k, x in inputs.items()}
    batch = a["ids"].shape[0]
    ids = a["ids"].reshape(batch // P, EMB, QUADS, FIELDS).transpose(2, 1, 0, 3).reshape(P, batch // P, FIELDS)
    arrays = {"dense_t": a["dense_ctx"].T, "ids": ids}
    for f in range(FIELDS):
        arrays[f"tbl_{f}"] = a[f"tbl_{f}"]
    arrays["w_top1"] = a["W_top1"]
    arrays["b_top1"] = a["b_top1"].reshape(-1, P).T
    arrays["w_top2"] = a["W_top2"]
    arrays["b_top2"] = a["b_top2"].reshape(-1, P).T
    arrays["w_top3"] = a["W_top3"].reshape(-1, P).T
    arrays["w1"] = a["L0_rec_W1"]
    arrays["b1"] = a["L0_rec_b1"].reshape(HC, 1)
    arrays["w2"] = a["L0_rec_W2"].transpose(1, 2, 0)
    arrays["b2"] = a["L0_rec_b2"].reshape(HC, 1)
    arrays = {f"in_{k}": np.ascontiguousarray(x) for k, x in arrays.items()}
    ap = {k[3:]: nc.dram_tensor(k, x.shape, mybir.dt.from_np(x.dtype), kind="ExternalInput").ap()
          for k, x in arrays.items()}
    y = nc.dram_tensor("y", (1, batch), mybir.dt.float32, kind="ExternalOutput").ap()
    dlrm_tower(nc, ap["dense_t"], ap["ids"], [ap[f"tbl_{f}"] for f in range(FIELDS)], ap["w_top1"], ap["b_top1"],
               ap["w_top2"], ap["b_top2"], ap["w_top3"], ap["w1"], ap["b1"], ap["w2"], ap["b2"], y)
    r = run_bass_kernel_spmd(nc, [arrays], core_ids=[0])
    return r.results[0]["y"].reshape(batch, 1)
```

```python
import concourse.bass as bass
from concourse import mybir
from contextlib import ExitStack

FIELDS = 26
EMB = 32
HC = 128
P = 128
QUADS = P // EMB
SLOTS = 2
RING = 4
HALF = FIELDS // 2
B1, B2 = 7, HALF - 7
VARS = FIELDS + 1
ONE = HALF
VW0 = HALF + 1
LOOKS = 3
LOOK0 = FIELDS - LOOKS
CUTS = 3
DENSE_CUTS = ((0, 0), (0, 1), (0, 2), None, (1, 0), (1, 1), (2, 0), (2, 1))
DENSE_PIECES = 2 * len(DENSE_CUTS) - DENSE_CUTS.count(None)


def tri(n):
    return n * (n + 1) // 2


def tri_row(n, a):
    return a * n - a * (a - 1) // 2


U_T1 = 0
U_T2 = U_T1 + tri(B1)
U_11 = U_T2 + tri(B2)
U_X = U_11 + 1
U_1U = U_X + B1 * B2
U_ROWS = U_1U + HALF
W_T1 = 0
W_T2 = W_T1 + tri(B1)
W_X = W_T2 + tri(B2)
W_ROWS = W_X + B1 * B2
COL_W = U_ROWS
COL_X = COL_W + W_ROWS
COLS = COL_X + HALF * HALF
U_TO_U = 22
U_TO_W = U_X - U_TO_U
W_TO_W = P - W_ROWS - U_TO_W
W_TO_P = W_X - W_TO_W
P_PER = P // W_TO_P
P_TILES = -(-HALF // P_PER)
X_PER = P // HALF
X_TO_U = P - U_ROWS
X_TO_W = (HALF - X_PER) * HALF - X_TO_U
FIRST_U = 0
FIRST_W = FIRST_U + 1 + HALF
FIRST_P = FIRST_W + HALF + 1
TILE_X = FIRST_P + P_TILES
M_TILES = TILE_X + 1
ONE_U, ONE_W = FIRST_U, FIRST_P - 1


def m_rows(m):
    if m == TILE_X:
        return X_PER * HALF
    if m >= FIRST_P:
        return W_TO_P * min(P_PER, HALF - P_PER * (m - FIRST_P))
    if m == ONE_W:
        return W_ROWS + X_TO_W
    return U_ROWS + U_TO_U if ONE_U < m < FIRST_W else P


def x_pieces():
    pieces = []
    for w in range(HALF):
        at = w * HALF
        for tile, lane, lo, hi in ((TILE_X, 0, 0, X_PER * HALF),
                                   (ONE_U, U_ROWS, X_PER * HALF, X_PER * HALF + X_TO_U),
                                   (ONE_W, W_ROWS, X_PER * HALF + X_TO_U, HALF * HALF)):
            u0, u1 = max(lo - at, 0), min(hi - at, HALF)
            if u0 < u1:
                pieces.append((w, u0, u1, tile, lane + at + u0 - lo))
    return pieces


PER_BANK = 512 // (VARS * QUADS)
BANKS = EMB // PER_BANK
FILLS = 2 * BANKS


def dlrm_tower(nc, dense_in, scratch, ids, look_ids, tables, w_top1, b_top1, w_top2, b_top2, w_top3, w1, b1, w2, b2,
               y):
    fp32 = mybir.dt.float32
    fp32r = mybir.dt.float32r
    bf16 = mybir.dt.bfloat16
    i32 = mybir.dt.int32
    ALU = mybir.AluOpType
    ACT = mybir.ActivationFunctionType

    batch = ids.shape[1] * P
    tiles = batch // P
    n_dense = w_top1.shape[0] - 2 * HC
    rows = P
    m1 = w_top1.shape[1] // P
    m2 = w_top2.shape[1] // P
    look_per = [-(-tables[LOOK0 + f].shape[0] // P) for f in range(LOOKS)]
    look_parts = tables[LOOK0].shape[0] // look_per[0]
    look_at = [sum(look_per[:f]) for f in range(LOOKS)]
    look_rows_all = sum(look_per)
    assert FILLS % RING == 0 and tiles % SLOTS == 0 and 2 * HC + n_dense == w_top1.shape[0]
    assert X_TO_W <= P - W_ROWS and P_TILES + 2 <= HALF
    assert all(look_per[f] * look_parts == tables[LOOK0 + f].shape[0] for f in range(LOOKS)) and LOOK0 >= HALF
    assert COLS <= 512 and m1 * rows <= 512 and m2 * P <= 512 and n_dense * len(DENSE_CUTS) == P

    ctx = ExitStack()
    with ctx:
        def sb(name, shape, dt=fp32):
            return ctx.enter_context(nc.sbuf_tensor(name, shape, dt))

        def ps(name, shape):
            return ctx.enter_context(nc.psum_tensor(name, shape, fp32))

        def sem(name):
            return ctx.enter_context(nc.semaphore(name))

        ids_all = sb("ids_all", [P, tiles, FIELDS], i32)
        idx = [sb(f"idx{s}", [P, FIELDS], i32) for s in range(SLOTS)]
        gath = [sb(f"gath{s}", [P, FIELDS, EMB]) for s in range(SLOTS)]
        look_ids_sb = sb("look_ids_sb", [P, LOOKS, rows], i32)
        look_rows = sb("look_rows", [P, look_rows_all], i32)
        look_cuts = sb("look_cuts", [P, look_rows_all, CUTS, EMB], bf16)
        hits = sb("hits", [P, look_rows_all, rows], bf16)
        emb_t = [sb(f"emb_t{s}", [P, EMB, VARS]) for s in range(SLOTS)]
        diag = [sb(f"diag{s}", [P, EMB, VARS, QUADS]) for s in range(SLOTS)]
        v_space = sb("v_space", [P, FIELDS * COLS])
        v = v_space[:, :].rearrange("p (j c) -> p j c", c=COLS)
        prod = [[sb("prod_u0", [P, EMB, U_ROWS])[:, :, :], sb("prod_w0", [P, EMB, W_ROWS])[:, :, :]],
                [sb("prod_u1", [P, EMB, U_ROWS])[:, :, :],
                 v_space[:, 0:EMB * W_ROWS].rearrange("p (c x) -> p c x", x=W_ROWS)]]
        mom = sb("mom", [P, M_TILES, rows])
        inner = [sb("inner_u", [U_X, HALF, rows]), sb("inner_w", [W_X, HALF, rows])]
        fold_w = sb("fold_w", [P, M_TILES, HC])
        w1_pairs = sb("w1_pairs", [P, COLS])
        w2_sb = fold_w[:, 0:FIELDS, :]
        b2_sb = sb("b2_sb", [P, 1])
        b2_k = sb("b2_k", [P, 1])
        ident = sb("ident", [P, P])
        wt1 = sb("wt1", [P, 2, m1 * P])
        wt1_dense = sb("wt1_dense", [P, m1 * P], bf16)
        dense = sb("dense", [P, batch], bf16)
        wt2_hi = sb("wt2_hi", [P, m1, m2 * P], fp32r)
        wt2_lo = sb("wt2_lo", [P, m1, m2 * P], fp32r)
        wt3 = sb("wt3", [P, m2 * P])
        bt1 = sb("bt1", [P, m1])
        bt2 = sb("bt2", [P, m2 * P])
        z_sb = sb("z_sb", [P, 2, rows])
        h1_sb = sb("h1_sb", [P, m1, rows])
        h1_hi = sb("h1_hi", [P, m1, rows], fp32r)
        h1_lo = sb("h1_lo", [P, m1, rows], fp32r)
        h2_sb = sb("h2_sb", [P, m2 * P])
        y_sb = sb("y_sb", [P, tiles])
        spare = mom[:, :, :].rearrange("p m b -> p (m b)")
        place = [0]

        def early(parts, size):
            place[0] += size
            return spare[0:parts, place[0] - size:place[0]]

        w1_sb = early(P, FIELDS * FIELDS).rearrange("p (i j) -> p i j", j=FIELDS)
        look_rest = early(P, look_rows_all * EMB).rearrange("p (i k) -> p i k", k=EMB)
        wt2_in = early(P, m1 * m2 * P).rearrange("p (k m) -> p k m", k=m1)
        chunks = P // n_dense
        width = [batch // chunks, m1 * P // chunks]
        dense_rest = early(P, sum(width))
        dense_cuts = early(P, CUTS * sum(width) // 2).bitcast(bf16).rearrange("p (c x) -> p c x", c=CUTS)

        bank = [ps(f"bank{i}", [P, 512]) for i in range(RING)]
        z_ps = ps("z_ps", [P, 2, rows])
        h1_ps = ps("h1_ps", [P, m1, rows])
        h2_ps = ps("h2_ps", [P, m2 * P])
        look_ps = ps("look_ps", [P, LOOKS, CUTS, EMB])

        ids_loaded = sem("ids_loaded")
        w1_loaded = sem("w1_loaded")
        w2_loaded = sem("w2_loaded")
        mlp_loaded = sem("mlp_loaded")
        dense_loaded = sem("dense_loaded")
        wt2_loaded = sem("wt2_loaded")
        look_table_loaded = sem("look_table_loaded")
        look_ids_loaded = sem("look_ids_loaded")
        consts_set = sem("consts_set")
        ident_zeroed = sem("ident_zeroed")
        ident_set = sem("ident_set")
        w1_diag_set = sem("w1_diag_set")
        w1_summed = sem("w1_summed")
        v_filled = sem("v_filled")
        v_copied = sem("v_copied")
        v_added = sem("v_added")
        v_joined = sem("v_joined")
        wt_filled = sem("wt_filled")
        wt_copied = sem("wt_copied")
        b2_scaled = sem("b2_scaled")
        look_rows_set = sem("look_rows_set")
        cut_made = sem("cut_made")
        rest_made = sem("rest_made")
        dense_cut = sem("dense_cut")
        wt1_dense_zeroed = sem("wt1_dense_zeroed")
        dense_left = sem("dense_left")
        dense_written = sem("dense_written")
        dense_placed = sem("dense_placed")
        wt2_cut = sem("wt2_cut")
        idx_staged = sem("idx_staged")
        tile_begun = sem("tile_begun")
        gathered_u = [sem(f"gathered_u{s}") for s in range(SLOTS)]
        gathered_w = [sem(f"gathered_w{s}") for s in range(SLOTS)]
        hits_ready = sem("hits_ready")
        looked_up = sem("looked_up")
        look_copied = sem("look_copied")
        transposed = sem("transposed")
        diag_ready = sem("diag_ready")
        prod_ready = [sem("prod_u_ready"), sem("prod_w_ready")]
        bank_filled = sem("bank_filled")
        bank_emptied = sem("bank_emptied")
        u_moved = sem("u_moved")
        w_moved = sem("w_moved")
        p_moved = sem("p_moved")
        x_moved = sem("x_moved")
        z_filled = sem("z_filled")
        z_copied = sem("z_copied")
        h1_filled = sem("h1_filled")
        h1_ready = sem("h1_ready")
        h1_hi_ready = sem("h1_hi_ready")
        h1_lo_ready = sem("h1_lo_ready")
        h2_filled = sem("h2_filled")
        h2_copied = sem("h2_copied")
        y_weighed = sem("y_weighed")
        y_ready = sem("y_ready")
        y_stored = sem("y_stored")

        W1_LOADS, MLP_LOADS = 2, 4
        CONSTS = 3 * SLOTS
        X_EARLY = 10
        PARTS = 2

        joined_u = v[:, HALF:, COL_X:COL_X + U_ROWS + U_TO_U]
        joined_w = v[:, 0:HALF, COL_X:COL_X + P]
        joined_p = v[:, 0:P_TILES, 0:P_PER * W_TO_P]
        joined_1u, joined_1w = v[:, P_TILES, 0:m_rows(ONE_U)], v[:, P_TILES + 1, 0:m_rows(ONE_W)]
        sources = [joined_1u] + [joined_u[:, w, :] for w in range(HALF)] \
            + [joined_w[:, u, :] for u in range(HALF)] + [joined_1w] \
            + [joined_p[:, p, 0:m_rows(FIRST_P + p)] for p in range(P_TILES)] \
            + [w1_pairs[:, COL_X:COL_X + m_rows(TILE_X)]]
        lots = []
        for m, source in enumerate(sources):
            if lots and lots[-1][0] == m_rows(m) and len(lots[-1][2]) < 4:
                lots[-1][2].append(source)
            else:
                lots.append((m_rows(m), m, [source]))

        TRIANGLES = ((U_T1, B1, 0), (U_T2, B2, B1), (COL_W + W_T1, B1, HALF), (COL_W + W_T2, B2, HALF + B1))

        block = ctx.enter_context(nc.Block())

        @block.sync
        def _(sp):
            sp.dma_start(ids_all[:, :, :], ids).then_inc(ids_loaded, 16)
            sp.dma_start(w1_sb[:, :, :], w1).then_inc(w1_loaded, 16)
            sp.dma_start(w1_pairs[:, U_11:U_11 + 1], b1).then_inc(w1_loaded, 16)
            sp.dma_start(w2_sb[:, :, :], w2).then_inc(w2_loaded, 16)
            sp.dma_start(b2_sb[:, :], b2).then_inc(w2_loaded, 16)
            for f in range(LOOKS):
                sp.dma_start(look_rest[0:look_parts, look_at[f]:look_at[f] + look_per[f], :],
                             tables[LOOK0 + f].rearrange("(p i) k -> p i k", p=look_parts)).then_inc(
                                 look_table_loaded, 16)

            def load_look_ids(t):
                sp.dma_start(look_ids_sb[:, :, :],
                             look_ids[bass.ds(t, 1), :, :].broadcast_to([P, LOOKS, rows])).then_inc(
                                 look_ids_loaded, 16)

            load_look_ids(0)
            sp.dma_start(dense_rest, dense_in).then_inc(dense_loaded, 16)
            sp.dma_start(wt2_in, w_top2.rearrange("(k p) m -> p k m", p=P)).then_inc(wt2_loaded, 16)
            sp.dma_start(wt1[:, :, :], w_top1[0:2 * HC, :].rearrange("(k p) m -> p k m", p=P)).then_inc(mlp_loaded, 16)
            sp.dma_start(wt3[:, :], w_top3.broadcast_to([P, m2 * P])).then_inc(mlp_loaded, 16)
            sp.dma_start(bt1[:, :], b_top1).then_inc(mlp_loaded, 16)
            sp.dma_start(bt2[:, :], b_top2.broadcast_to([P, m2 * P])).then_inc(mlp_loaded, 16)

            def move(tile, lane, src, signal):
                sp.dma_start(mom[lane:lane + src.shape[0], tile, :], src).then_inc(signal, 16)

            def move_x(pieces):
                for w, u0, u1, tile, lane in pieces:
                    sp.dma_start(mom[lane:lane + u1 - u0, tile, :],
                                 mom[U_1U + u0:U_1U + u1, FIRST_U + 1 + w, :]).then_inc(x_moved, 16)

            def move_u(t):
                sp.wait_ge(bank_emptied, PARTS * (FILLS * t + BANKS))
                move(slice(FIRST_U + 1, FIRST_W), U_ROWS, inner[0][0:U_TO_U, :, :], u_moved)
                move(slice(FIRST_W, FIRST_P - 1), W_ROWS, inner[0][U_TO_U:U_X, :, :], w_moved)
                move_x(x_pieces()[:X_EARLY])

            def move_w(t):
                sp.wait_ge(bank_emptied, PARTS * FILLS * (t + 1))
                move(slice(FIRST_W, FIRST_P - 1), W_ROWS + U_TO_W, inner[1][0:W_TO_W, :, :], w_moved)
                for k in range(P_PER):
                    n = len(range(k, HALF, P_PER))
                    move(slice(FIRST_P, FIRST_P + n), k * W_TO_P, inner[1][W_TO_W:W_X, k::P_PER, :], p_moved)
                move_x(x_pieces()[X_EARLY:])

            def next_look_ids(t):
                sp.wait_ge(hits_ready, LOOKS * t)
                load_look_ids(t)

            def tile(t):
                if not (isinstance(t, int) and t + 2 >= tiles):
                    next_look_ids(t + 2)
                move_u(t)
                move_w(t)

            for part in range(CUTS):
                sp.wait_ge(dense_cut, part + 1)
                sp.dma_start(scratch[part], dense_cuts[:, part, :]).then_inc(dense_written, 16)
            next_look_ids(1)
            sp.wait_ge(dense_written, 16 * CUTS)
            sp.wait_ge(wt1_dense_zeroed, 1)
            for slot, parts in enumerate(DENSE_CUTS):
                q = slice(slot * n_dense, (slot + 1) * n_dense)
                for out, i, x in ((dense, 0, slice(0, width[0])), (wt1_dense, 1, slice(width[0], sum(width)))):
                    if parts is not None or i == 0:
                        sp.dma_start(out[q, :].rearrange("n (c x) -> n c x", c=chunks),
                                     scratch[parts[i] if parts else 0, :, x].rearrange(
                                         "(c n) x -> n c x", n=n_dense)).then_inc(dense_placed, 16)
            move_u(0)
            move_w(0)
            next_look_ids(2)
            with sp.Fori(1, tiles - 2) as t:
                tile(t)
            tile(tiles - 2)
            tile(tiles - 1)
            sp.wait_ge(y_ready, tiles)
            sp.dma_start(y, y_sb[:, :]).then_inc(y_stored, 16)
            sp.wait_ge(y_stored, 16)

        @block.gpsimd
        def _(pool):
            def gather(t, s, free):
                if free is not None:
                    pool.wait_ge(transposed, free)
                nc.gpsimd.tensor_copy(idx[s][:, :], ids_all[:, t, :]).then_inc(idx_staged, 1)
                pool.wait_ge(idx_staged, t + 1)
                pool.sem_inc(tile_begun, 1)
                for f in range(HALF):
                    nc.gpsimd.indirect_dma_start(
                        gath[s][:, f, :], None, tables[f],
                        bass.IndirectOffsetOnAxis(idx[s][:, f:f + 1], 0)).then_inc(gathered_u[s], 16)
                for f in range(HALF, LOOK0):
                    nc.gpsimd.indirect_dma_start(
                        gath[s][:, f, :], None, tables[f],
                        bass.IndirectOffsetOnAxis(idx[s][:, f:f + 1], 0)).then_inc(gathered_w[s], 16)

            for f in range(LOOKS):
                nc.gpsimd.iota(look_rows[:, look_at[f]:look_at[f] + look_per[f]], pattern=[[1, look_per[f]]], base=0,
                               channel_multiplier=look_per[f]).then_inc(look_rows_set, 1)
            nc.gpsimd.memset(ident[:, :], 0.0).then_inc(ident_zeroed, 1)
            pool.wait_ge(ident_zeroed, 1)
            nc.gpsimd.affine_select(out=ident[:, :], in_=ident[:, :], compare_op=ALU.not_equal, fill=1.0, base=0,
                                    pattern=[[-1, P]], channel_multiplier=1).then_inc(ident_set, 1)
            pool.wait_ge(ids_loaded, 16)
            for s in range(SLOTS):
                gather(s, s, None)
            with pool.Fori(1, tiles // SLOTS) as n:
                for s in range(SLOTS):
                    gather(SLOTS * n + s, s, 2 * (SLOTS * (n - 1) + s + 1))

        @block.scalar
        def _(act):
            act.wait_ge(w1_loaded, 16 * W1_LOADS)
            for first, size, field in TRIANGLES:
                for a in range(size):
                    col = first + tri_row(size, a)
                    last = nc.scalar.copy(w1_pairs[:, col:col + 1], w1_sb[:, field + a, field + a:field + a + 1])
            last.then_inc(w1_diag_set, 1)
            act.wait_ge(w2_loaded, 32)
            nc.scalar.mul(b2_k[:, :], b2_sb[:, :], float(EMB)).then_inc(b2_scaled, 1)
            for j in range(FIELDS):
                act.wait_ge(v_filled, j + 1)
                nc.scalar.copy(v[:, j, :], bank[j % RING][:, 0:COLS]).then_inc(v_copied, 1)

            def copy_fold_w():
                for k, (size, at, sources) in enumerate(lots):
                    act.wait_ge(wt_filled, k + 1)
                    nc.scalar.copy(fold_w[0:size, at:at + len(sources), :],
                                   bank[k % RING][0:size, 0:len(sources) * HC].rearrange(
                                       "p (j h) -> p j h", h=HC)).then_inc(wt_copied, 1)

            act.wait_ge(mlp_loaded, 16 * MLP_LOADS)
            act.wait_ge(b2_scaled, 1)

            def empty_banks(t, i):
                for k in range(BANKS):
                    fill = BANKS * i + k
                    act.wait_ge(bank_filled, FILLS * t + fill + 1)
                    at = k * PER_BANK * QUADS
                    src = bank[fill % RING][:, 0:PER_BANK * VARS * QUADS].rearrange(
                        "p (g j r) -> p j g r", j=VARS, r=QUADS)
                    size, first, own, same = [(U_ROWS, FIRST_U, slice(ONE, VARS), slice(0, ONE)),
                                              (W_ROWS, FIRST_W, slice(0, ONE + 1), slice(VW0, VARS))][i]
                    dst = mom[0:size, first:first + HALF + 1, at:at + PER_BANK * QUADS]
                    nc.scalar.copy(dst.rearrange("p j (g r) -> p j g r", r=QUADS),
                                   src[0:size, own]).then_inc(bank_emptied, 1)
                    size = [U_X, W_X][i]
                    dst = inner[i][0:size, :, at:at + PER_BANK * QUADS]
                    nc.scalar.copy(dst.rearrange("p j (g r) -> p j g r", r=QUADS),
                                   src[0:size, same]).then_inc(bank_emptied, 1)

            def relu_h1(t):
                act.wait_ge(h1_filled, t + 1)
                if not (isinstance(t, int) and t == 0):
                    act.wait_ge(h1_lo_ready, 2 * t)
                    act.wait_ge(h2_filled, t)
                for half in range(2):
                    these = slice(half * m1 // 2, (half + 1) * m1 // 2)
                    for m in range(m1)[these]:
                        last = nc.scalar.activation(h1_sb[:, m, :], h1_ps[:, m, :], ACT.Relu, bias=bt1[:, m:m + 1])
                    last.then_inc(h1_ready, 1)
                    act.wait_ge(h1_ready, 2 * t + half + 1)
                    nc.scalar.copy(h1_hi[:, these, :], h1_sb[:, these, :]).then_inc(h1_hi_ready, 1)

            def copy_z(t):
                act.wait_ge(z_filled, t + 1)
                nc.scalar.copy(z_sb[:, 0, :], z_ps[:, 0, :])
                nc.scalar.activation(z_sb[:, 1, :], z_ps[:, 1, :], ACT.Identity, bias=b2_k[:, :]).then_inc(z_copied, 1)

            act.wait_ge(cut_made, CUTS)
            act.wait_ge(dense_written, 16 * CUTS)
            act.wait_ge(wt2_cut, 2)
            for i in range(2):
                empty_banks(0, i)
            act.wait_ge(v_added, 2)
            nc.scalar.copy(joined_u[:, :, 0:U_ROWS], v[:, HALF:, 0:U_ROWS])
            nc.scalar.copy(joined_u[:, :, U_ROWS:], v[:, 0:HALF, 0:U_TO_U]).then_inc(v_joined, 1)
            copy_fold_w()
            copy_z(0)

            def tile(t):
                act.wait_ge(z_filled, t)
                empty_banks(t, 0)
                empty_banks(t, 1)
                relu_h1(t - 1)
                copy_z(t)

            with act.Fori(1, tiles) as t:
                tile(t)
            relu_h1(tiles - 1)

        @block.vector
        def _(dve):
            nc.vector.memset(w1_pairs[:, U_1U:U_ROWS], 0.0)
            nc.vector.memset(wt1_dense[:, :], 0.0).then_inc(wt1_dense_zeroed, 1)

            def set_consts(s):
                nc.vector.memset(emb_t[s][:, :, ONE:VW0], 1.0).then_inc(consts_set, 1)
                nc.vector.memset(prod[s][0][:, :, U_11:U_X], 1.0).then_inc(consts_set, 1)
                nc.vector.memset(diag[s][:, :, :, :], 0.0).then_inc(consts_set, 1)

            set_consts(1)

            dve.wait_ge(w1_loaded, 16 * W1_LOADS)
            for first, pf in ((U_X, 0), (COL_W + W_X, HALF)):
                qf = pf + B1
                nc.vector.tensor_tensor(
                    w1_pairs[:, first:first + B1 * B2].rearrange("p (a b) -> p a b", b=B2),
                    w1_sb[:, pf:qf, qf:qf + B2],
                    w1_sb[:, qf:qf + B2, pf:qf].rearrange("p b a -> p a b"), ALU.add)
            nc.vector.tensor_tensor(
                w1_pairs[:, COL_X:].rearrange("p (w u) -> p w u", u=HALF), w1_sb[:, HALF:, 0:HALF],
                w1_sb[:, 0:HALF, HALF:].rearrange("p u w -> p w u"), ALU.add)
            for first, size, field in TRIANGLES:
                for a in range(size - 1):
                    col = first + tri_row(size, a) + 1
                    f = field + a
                    last = nc.vector.tensor_tensor(
                        w1_pairs[:, col:col + size - 1 - a], w1_sb[:, f, f + 1:field + size],
                        w1_sb[:, f + 1:field + size, f], ALU.add)
            last.then_inc(w1_summed, 1)

            def fold():
                cross = v[:, :, COL_X:].rearrange("p j (w u) -> p j w u", u=HALF)
                x_u = v[:, :, U_X:U_1U].rearrange("p j (a b) -> p j a b", b=B2)
                x_w = v[:, :, COL_W + W_X:COL_X].rearrange("p j (a b) -> p j a b", b=B2)
                first, second = [], []
                for t1, t2, f, x, across in ((U_T1, U_T2, 0, x_u, cross),
                                             (COL_W + W_T1, COL_W + W_T2, HALF, x_w,
                                              cross.rearrange("p j w u -> p j u w"))):
                    g = HALF - f
                    others = slice(g, g + HALF)
                    for t, n, lo in ((t1, B1, 0), (t2, B2, B1)):
                        for a in range(n):
                            at = t + tri_row(n, a)
                            first.append((v[:, others, at:at + n - a], across[:, f + lo + a, :, lo + a:lo + n]))
                            if a + 1 < n:
                                second.append((v[:, others, at + 1:at + n - a],
                                               across[:, f + lo + a + 1:f + lo + n, :, lo + a].rearrange(
                                                   "p b o -> p o b")))
                    first.append((x[:, others, :, :], across[:, f + B1:f + HALF, :, 0:B1].rearrange(
                        "p b o a -> p o a b")))
                    second.append((x[:, others, :, :], across[:, f:f + B1, :, B1:HALF].rearrange(
                        "p a o b -> p o a b")))
                    for a in range(B1):
                        at = t1 + tri_row(B1, a)
                        outer = slice(f + B1, f + HALF)
                        first.append((v[:, outer, at:at + B1 - a],
                                      x[:, f + a:f + B1, a, :].rearrange("p m b -> p b m")))
                        if a + 1 < B1:
                            second.append((v[:, outer, at + 1:at + B1 - a],
                                           x[:, f + a, a + 1:, :].rearrange("p m b -> p b m")))
                    for b in range(B2):
                        at = t2 + tri_row(B2, b)
                        outer = slice(f, f + B1)
                        first.append((v[:, outer, at:at + B2 - b],
                                      x[:, f + B1 + b:f + HALF, :, b].rearrange("p m a -> p a m")))
                        if b + 1 < B2:
                            second.append((v[:, outer, at + 1:at + B2 - b], x[:, f + B1 + b, :, b + 1:]))
                dve.wait_ge(v_copied, FIELDS)
                for kept, left in first:
                    last = nc.vector.tensor_tensor(kept, kept, left, ALU.add)
                last.then_inc(v_added, 1)
                dve.wait_ge(v_added, 1)
                for kept, left in second:
                    last = nc.vector.tensor_tensor(kept, kept, left, ALU.add)
                last.then_inc(v_added, 1)
                dve.wait_ge(v_added, 2)
                v_u, v_w = v[:, 0:HALF, :], v[:, HALF:, :]
                nc.vector.tensor_copy(joined_w[:, :, 0:W_ROWS], v_u[:, :, COL_W:COL_X])
                nc.vector.tensor_copy(joined_w[:, :, W_ROWS:W_ROWS + U_TO_W], v_u[:, :, U_TO_U:U_X])
                nc.vector.tensor_copy(joined_w[:, :, W_ROWS + U_TO_W:],
                                      v_w[:, :, COL_W:COL_W + W_TO_W]).then_inc(v_joined, 1)
                dve.wait_ge(v_joined, 2)
                x0 = COL_X + m_rows(TILE_X)
                for out, own, x in ((joined_1u, slice(0, U_ROWS), slice(x0, x0 + X_TO_U)),
                                    (joined_1w, slice(COL_W, COL_X), slice(x0 + X_TO_U, COLS))):
                    n = own.stop - own.start
                    nc.vector.tensor_copy(out[:, 0:n], w1_pairs[:, own])
                    nc.vector.tensor_copy(out[:, n:], w1_pairs[:, x])
                for k in range(P_PER):
                    n = len(range(k, HALF, P_PER))
                    last = nc.vector.tensor_copy(joined_p[:, 0:n, k * W_TO_P:(k + 1) * W_TO_P],
                                                 v_w[:, k::P_PER, COL_W + W_TO_W:COL_W + W_X])
                last.then_inc(v_joined, 1)

            def cut_bf16(value, part, made, left):
                for i in range(CUTS):
                    if i:
                        dve.wait_ge(made, i)
                        nc.vector.tensor_tensor(value, value, part(i - 1), ALU.subtract).then_inc(left, 1)
                        dve.wait_ge(left, i)
                    nc.vector.tensor_copy(part(i), value).then_inc(made, 1)

            def cut_look_tables():
                dve.wait_ge(look_table_loaded, 16 * LOOKS)
                cut_bf16(look_rest[0:look_parts, :, :], lambda i: look_cuts[0:look_parts, :, i, :],
                         cut_made, rest_made)

            def cut_dense():
                dve.wait_ge(dense_loaded, 16)
                cut_bf16(dense_rest, lambda i: dense_cuts[:, i, :], dense_cut, dense_left)

            def cut_wt2():
                dve.wait_ge(wt2_loaded, 16)
                nc.vector.tensor_copy(wt2_hi[:, :, :], wt2_in).then_inc(wt2_cut, 1)
                dve.wait_ge(wt2_cut, 1)
                nc.vector.tensor_tensor(wt2_lo[:, :, :], wt2_in, wt2_hi[:, :, :].bitcast(fp32),
                                        ALU.subtract).then_inc(wt2_cut, 1)

            def cut_h1(t):
                for half in range(2):
                    these = slice(half * m1 // 2, (half + 1) * m1 // 2)
                    dve.wait_ge(h1_hi_ready, 2 * t + half + 1)
                    nc.vector.tensor_tensor(h1_lo[:, these, :], h1_sb[:, these, :], h1_hi[:, these, :].bitcast(fp32),
                                            ALU.subtract).then_inc(h1_lo_ready, 1)

            def last_layer(t):
                dve.wait_ge(h2_filled, t + 1)
                if not (isinstance(t, int) and t == 0):
                    dve.wait_ge(y_ready, t)
                nc.vector.tensor_tensor(h2_sb[:, :], h2_ps[:, :], bt2[:, :], ALU.add).then_inc(h2_copied, 1)
                dve.wait_ge(h2_copied, t + 1)
                nc.vector.scalar_tensor_tensor(h2_sb[:, :], h2_sb[:, :], 0.0, wt3[:, :], ALU.max,
                                               ALU.mult).then_inc(y_weighed, 1)
                dve.wait_ge(y_weighed, t + 1)
                nc.vector.tensor_reduce(y_sb[:, bass.ds(t, 1)], h2_sb[:, :], mybir.AxisListType.X,
                                        ALU.add).then_inc(y_ready, 1)

            def find(t):
                dve.wait_ge(look_ids_loaded, 16 * (t + 1))
                for f in range(LOOKS):
                    shape = [look_parts, look_per[f], rows]
                    these = slice(look_at[f], look_at[f] + look_per[f])
                    nc.vector.tensor_tensor(
                        hits[0:look_parts, these, :], look_ids_sb[0:look_parts, f:f + 1, :].broadcast_to(shape),
                        look_rows[0:look_parts, these].unsqueeze(2).broadcast_to(shape),
                        ALU.is_equal).then_inc(hits_ready, 1)

            def tile_in(t, s, turn, free):
                for half, gathered, field, at in ((0, gathered_u, 0, 0), (1, gathered_w, HALF, VW0)):
                    if half:
                        dve.wait_ge(looked_up, t + 1)
                        nc.vector.tensor_reduce(gath[s][:, LOOK0:LOOK0 + LOOKS, :],
                                                look_ps[:, :, :, :].rearrange("p f c k -> p f k c"),
                                                mybir.AxisListType.X, ALU.add).then_inc(look_copied, 1)
                    dve.wait_ge(gathered[s], 16 * (HALF - half * LOOKS) * (turn + 1))
                    if half:
                        dve.wait_ge(look_copied, t + 1)
                    nc.vector.transpose(emb_t[s][:, :, at:at + HALF].rearrange("p c j -> p j c"),
                                        gath[s][:, field:field + HALF, :]).then_inc(transposed, 1)
                    dve.wait_ge(transposed, 2 * t + half + 1)
                    if free is not None and half == 0:
                        dve.wait_ge(bank_filled, free)
                    places = slice(at, at + HALF) if half else slice(at, ONE + 1)
                    for r in range(QUADS):
                        q = slice(EMB * r, EMB * (r + 1))
                        nc.vector.tensor_copy(diag[s][q, :, places, r], emb_t[s][q, :, places]).then_inc(
                            diag_ready, 1)
                    if half == 0:
                        products_u(s)
                if isinstance(t, int) and t == 1:
                    dve.wait_ge(wt_filled, len(lots))
                products_w(s)

            def products(s, i, t1, t2, x, at):
                e = emb_t[s]
                out = prod[s][i]
                for t, n, lo in ((t1, B1, at), (t2, B2, at + B1)):
                    for a in range(n):
                        col = t + tri_row(n, a)
                        nc.vector.tensor_tensor(
                            out[:, :, col:col + n - a], e[:, :, lo + a:lo + a + 1].broadcast_to([P, EMB, n - a]),
                            e[:, :, lo + a:lo + n], ALU.mult)
                last = nc.vector.tensor_tensor(
                    out[:, :, x:x + B1 * B2].rearrange("p c (a b) -> p c a b", b=B2),
                    e[:, :, at:at + B1].unsqueeze(3).broadcast_to([P, EMB, B1, B2]),
                    e[:, :, at + B1:at + HALF].unsqueeze(2).broadcast_to([P, EMB, B1, B2]), ALU.mult)
                if i == 0:
                    last = nc.vector.tensor_copy(out[:, :, U_1U:U_ROWS], e[:, :, 0:HALF])
                last.then_inc(prod_ready[i], 1)

            def products_u(s):
                products(s, 0, U_T1, U_T2, U_X, 0)

            def products_w(s):
                products(s, 1, W_T1, W_T2, W_X, VW0)

            set_consts(0)
            cut_look_tables()
            dve.wait_ge(look_rows_set, LOOKS)
            find(0)
            cut_dense()
            cut_wt2()
            dve.wait_ge(consts_set, CONSTS)
            tile_in(0, 0, 0, None)
            fold()
            find(1)
            tile_in(1, 1, 0, None)
            find(2)
            dve.wait_ge(mlp_loaded, 16 * MLP_LOADS)

            def tile(t, s, turn, free):
                tile_in(t, s, turn, free)
                if not (isinstance(t, int) and t + 1 == tiles):
                    find(t + 1)
                if not (isinstance(t, int) and t < 3):
                    last_layer(t - 3)
                cut_h1(t - 2)

            for s in range(SLOTS):
                tile(SLOTS + s, s, 1, FILLS * (s + 1))
            with dve.Fori(2, tiles // SLOTS - 1) as n:
                for s in range(SLOTS):
                    tile(SLOTS * n + s, s, n, FILLS * (SLOTS * (n - 1) + s + 1))
            for s in range(SLOTS):
                tile(tiles - SLOTS + s, s, tiles // SLOTS - 1, FILLS * (tiles - 2 * SLOTS + s + 1))
            last_layer(tiles - 3)
            cut_h1(tiles - 2)
            last_layer(tiles - 2)
            cut_h1(tiles - 1)
            last_layer(tiles - 1)

        @block.tensor
        def _(pe):
            def transpose_fold_w():
                pe.wait_ge(v_joined, 3)
                pe.wait_ge(ident_set, 1)
                pe.wait_ge(bank_emptied, PARTS * FILLS)
                for k, (size, _, sources) in enumerate(lots):
                    if k >= RING:
                        pe.wait_ge(wt_copied, k - RING + 1)
                    for g, src in enumerate(sources):
                        last = nc.tensor.transpose(bank[k % RING][0:size, g * HC:(g + 1) * HC], src, ident[:, :])
                    last.then_inc(wt_filled, 1)
                pe.wait_ge(wt_copied, len(lots))

            def look_up(t):
                pe.wait_ge(hits_ready, LOOKS * (t + 1))
                if isinstance(t, int) and t == 0:
                    pe.wait_ge(cut_made, CUTS)
                else:
                    pe.wait_ge(look_copied, t)
                for f in range(LOOKS):
                    for i in range(look_per[f]):
                        last = nc.tensor.matmul(look_ps[:, f, :, :], hits[0:look_parts, look_at[f] + i, :],
                                                look_cuts[0:look_parts, look_at[f] + i, :, :],
                                                start=(i == 0), stop=(i == look_per[f] - 1))
                last.then_inc(looked_up, 1)

            def moments(t, s, i):
                first = isinstance(t, int) and t == 0
                size = W_ROWS if i else U_ROWS
                if i == 0:
                    pe.wait_ge(diag_ready, 2 * QUADS * (t + 1))
                pe.wait_ge(prod_ready[i], t + 1)
                for k in range(BANKS):
                    fill = BANKS * i + k
                    if not (first and fill < RING):
                        pe.wait_ge(bank_emptied, PARTS * (FILLS * t + fill - RING + 1))
                    for g in range(PER_BANK):
                        at = g * VARS * QUADS
                        last = nc.tensor.matmul(bank[fill % RING][0:size, at:at + VARS * QUADS],
                                                prod[s][i][:, k * PER_BANK + g, :],
                                                diag[s][:, k * PER_BANK + g, :, :], start=True, stop=True)
                    last.then_inc(bank_filled, 1)

            cubic_u = list(range(FIRST_U + 1, FIRST_W))
            cubic_w = list(range(FIRST_W, FIRST_P - 1))
            cubic_p = list(range(FIRST_P, TILE_X))
            quadratic = [ONE_U, ONE_W, TILE_X]

            def contract(z, tiles_of_z, part):
                for m in part:
                    last = nc.tensor.matmul(z_ps[:, z, :], fold_w[0:m_rows(m), m, :], mom[0:m_rows(m), m, :],
                                            start=(m == tiles_of_z[0]), stop=(m == tiles_of_z[-1]))
                return last

            def contract_all(t):
                pe.wait_ge(bank_emptied, PARTS * (FILLS * t + BANKS))
                pe.wait_ge(u_moved, 16 * (t + 1))
                contract(1, cubic_u + cubic_w + cubic_p, cubic_u)
                pe.wait_ge(bank_emptied, PARTS * FILLS * (t + 1))
                pe.wait_ge(w_moved, 32 * (t + 1))
                contract(1, cubic_u + cubic_w + cubic_p, cubic_w)
                pe.wait_ge(p_moved, 16 * P_PER * (t + 1))
                contract(1, cubic_u + cubic_w + cubic_p, cubic_p)
                pe.wait_ge(x_moved, 16 * len(x_pieces()) * (t + 1))
                contract(0, quadratic, quadratic).then_inc(z_filled, 1)

            def layer1(t):
                pe.wait_ge(z_copied, t + 1)
                if not (isinstance(t, int) and t == 0):
                    pe.wait_ge(h1_ready, 2 * t)
                for m in range(m1):
                    cols = slice(m * P, (m + 1) * P)
                    for k in range(2):
                        nc.tensor.matmul(h1_ps[:, m, :], wt1[:, k, cols], z_sb[:, k, :], start=(k == 0), stop=False)
                    last = nc.tensor.matmul(h1_ps[:, m, :], wt1_dense[:, cols], dense[:, bass.ds(t * rows, rows)],
                                            start=False, stop=True)
                last.then_inc(h1_filled, 1)

            def layer2(t):
                if not (isinstance(t, int) and t == 0):
                    pe.wait_ge(h2_copied, t)
                for k in range(m1):
                    if k % (m1 // 2) == 0:
                        pe.wait_ge(h1_lo_ready, 2 * t + 2 * k // m1 + 1)
                    for part, (h, w) in enumerate(((h1_hi, wt2_hi), (h1_hi, wt2_lo), (h1_lo, wt2_hi))):
                        last = nc.tensor.matmul(h2_ps[:, :], h[:, k, :], w[:, k, :], start=(k == 0 and part == 0),
                                                stop=(k == m1 - 1 and part == 2))
                last.then_inc(h2_filled, 1)

            pe.wait_ge(w2_loaded, 32)
            pe.wait_ge(w1_diag_set, 1)
            pe.wait_ge(w1_summed, 1)
            for j in range(FIELDS):
                if j == HALF:
                    look_up(0)
                if j >= RING:
                    pe.wait_ge(v_copied, j - RING + 1)
                nc.tensor.matmul(bank[j % RING][:, 0:COLS], w2_sb[:, j, :], w1_pairs[:, :],
                                 start=True, stop=True).then_inc(v_filled, 1)
            pe.wait_ge(v_copied, FIELDS)
            for i in range(2):
                moments(0, 0, i)
            transpose_fold_w()
            look_up(1)
            contract_all(0)
            pe.wait_ge(mlp_loaded, 16 * MLP_LOADS)
            pe.wait_ge(dense_placed, 16 * DENSE_PIECES)
            pe.wait_ge(wt2_cut, 2)

            def tile(t, s):
                moments(t, s, 0)
                layer1(t - 1)
                moments(t, s, 1)
                if not (isinstance(t, int) and t < 2):
                    layer2(t - 2)
                if not (isinstance(t, int) and t + 1 == tiles):
                    look_up(t + 1)
                contract_all(t)

            tile(1, 1)
            with pe.Fori(1, tiles // SLOTS - 1) as n:
                for s in range(SLOTS):
                    tile(SLOTS * n + s, s)
            for s in range(SLOTS):
                tile(tiles - SLOTS + s, s)
            layer2(tiles - 2)
            layer1(tiles - 1)
            layer2(tiles - 1)


def kernel(**inputs):
    import numpy as np
    import concourse.bacc as bacc
    from concourse.bass_utils import run_bass_kernel_spmd

    nc = bacc.Bacc("TRN2", target_bir_lowering=False, num_devices=1)
    a = {k: np.asarray(x) for k, x in inputs.items()}
    batch = a["ids"].shape[0]
    order = sorted(range(FIELDS), key=lambda f: -a[f"tbl_{f}"].shape[0])
    tiles = batch // P
    ids = a["ids"][:, order].reshape(tiles, EMB, QUADS, FIELDS).transpose(2, 1, 0, 3).reshape(P, tiles, FIELDS)
    w_dense = a["W_top1"][2 * HC:]
    n_dense = w_dense.shape[0]
    dense = [x.reshape(n_dense, P // n_dense, -1).transpose(1, 0, 2).reshape(P, -1) for x in
             (a["dense_ctx"].T, w_dense)]
    arrays = {"dense": np.concatenate(dense, axis=1), "ids": ids, "look_ids": ids[:, :, LOOK0:].transpose(1, 2, 0)}
    for place, f in enumerate(order):
        arrays[f"tbl_{place}"] = a[f"tbl_{f}"]
    arrays["w_top1"] = a["W_top1"]
    arrays["b_top1"] = a["b_top1"].reshape(-1, P).T
    arrays["w_top2"] = a["W_top2"]
    arrays["b_top2"] = a["b_top2"].reshape(1, -1)
    arrays["w_top3"] = a["W_top3"].reshape(1, -1)
    arrays["w1"] = a["L0_rec_W1"][:, order][:, :, order]
    arrays["b1"] = a["L0_rec_b1"].reshape(HC, 1)
    arrays["w2"] = a["L0_rec_W2"][:, :, order].transpose(1, 2, 0)
    arrays["b2"] = a["L0_rec_b2"].reshape(HC, 1)
    arrays = {f"in_{k}": np.ascontiguousarray(x) for k, x in arrays.items()}
    ap = {k[3:]: nc.dram_tensor(k, x.shape, mybir.dt.from_np(x.dtype), kind="ExternalInput").ap()
          for k, x in arrays.items()}
    y = nc.dram_tensor("y", (P, tiles), mybir.dt.float32, kind="ExternalOutput").ap()
    scratch = nc.dram_tensor("scratch", (CUTS, *arrays["in_dense"].shape), mybir.dt.bfloat16, kind="Internal").ap()
    dlrm_tower(nc, ap["dense"], scratch, ap["ids"], ap["look_ids"], [ap[f"tbl_{f}"] for f in range(FIELDS)],
               ap["w_top1"], ap["b_top1"], ap["w_top2"], ap["b_top2"], ap["w_top3"], ap["w1"], ap["b1"], ap["w2"],
               ap["b2"], y)
    r = run_bass_kernel_spmd(nc, [arrays], core_ids=[0])
    return r.results[0]["y"].T.reshape(batch, 1)
```
